# Optimizing a Trainium2 kernel written in Bass

```python
import numpy as np
import jax
import jax.numpy as jnp

def _softmax(x, axis=-1):
    return jax.nn.softmax(x, axis=axis)

def _gelu(x):
    return jax.nn.gelu(x, approximate=True)

def _silu(x):
    return jax.nn.silu(x)

def _sigmoid(x):
    return jax.nn.sigmoid(x)

def _layernorm(x, axis=-1, eps=1e-05):
    m = jnp.mean(x, axis=axis, keepdims=True)
    v = jnp.var(x, axis=axis, keepdims=True)
    return (x - m) / jnp.sqrt(v + eps)

def _scatter_add(tgt, idx, src, axis=0):
    return tgt.at[idx].add(src)

def _segment_sum(src, seg, n):
    return jax.ops.segment_sum(src, seg, n)
kernel_name = 'mk_adj_preln_d4_adj_r2_ca2b1c'

def setup_inputs(seed: int=0):
    np.random.seed(seed)
    _w = jnp.asarray

    def _rec_inputs():
        import jax
        import jax.numpy as jnp
        _gk = jax.random.key(seed)
        x = -0.0005207 + 1.001 * jax.random.normal(jax.random.fold_in(_gk, 1), (8, 1024, 128), jnp.float32)
        _w = (1.0 + jnp.arange(1024, dtype=jnp.float32)) ** (-0.5)
        _w = _w / _w.mean()
        _pij = jnp.clip(0.0078125 * _w[:, None] * _w[None, :], 0.0, 1.0)
        _a = jax.random.uniform(jax.random.fold_in(_gk, 2), (1024, 1024)) < _pij
        adj = _a.astype(jnp.int32)
        return (x, adj)
    x, adj = _rec_inputs()

    def _L0_gnn_setup():
        import jax, jax.numpy as jnp
        import numpy as np
        import math
        CHUNK = 128
        NUM_HEADS = 4
        EPS = 1e-05
        key = jax.random.key(seed)
        ks = jax.random.split(key, 12)
        B, N, F = (4, 1024, 128)
        x = jax.random.normal(ks[0], (B, N, F), dtype=jnp.float32)
        adj_matrix = jax.random.randint(ks[1], (N, N), 0, 2, dtype=jnp.int32)
        s = 1.0 / math.sqrt(F)
        Wq = jax.random.normal(ks[2], (F, F), dtype=jnp.float32) * s
        bq = jnp.zeros((F,), dtype=jnp.float32)
        Wk = jax.random.normal(ks[3], (F, F), dtype=jnp.float32) * s
        bk = jnp.zeros((F,), dtype=jnp.float32)
        Wv = jax.random.normal(ks[4], (F, F), dtype=jnp.float32) * s
        bv = jnp.zeros((F,), dtype=jnp.float32)
        Wo = jax.random.normal(ks[5], (F, F), dtype=jnp.float32) * s
        bo = jnp.zeros((F,), dtype=jnp.float32)
        gamma = jnp.ones((F,), dtype=jnp.float32)
        beta = jnp.zeros((F,), dtype=jnp.float32)
        return {'x': x, 'adj_matrix': adj_matrix, 'Wq': Wq, 'bq': bq, 'Wk': Wk, 'bk': bk, 'Wv': Wv, 'bv': bv, 'Wo': Wo, 'bo': bo, 'gamma': gamma, 'beta': beta}
    _L0_gnn_all = _L0_gnn_setup()
    _L0_gnn_in = {k: v for k, v in _L0_gnn_all.items() if k in ('Wq', 'bq', 'Wk', 'bk', 'Wv', 'bv', 'Wo', 'bo', 'gamma', 'beta')}
    del _L0_gnn_all

    def _L1_gnn_setup():
        import jax, jax.numpy as jnp
        import numpy as np
        ALPHA = 0.2
        EPS = 1e-06
        key = jax.random.key(seed)
        ks = jax.random.split(key, 8)
        B, N, D, H = (2, 1024, 128, 8)
        dh = D // H
        x = jax.random.normal(ks[0], (B, N, D), dtype=jnp.float32)
        adj = jax.random.randint(ks[1], (N, N), 0, 2, dtype=jnp.int32)
        adj = jnp.maximum(adj, jnp.eye(N, dtype=jnp.int32))
        p = jax.random.uniform(ks[2], (B, N, N), dtype=jnp.float32)
        prior = p / jnp.sum(p, axis=-1, keepdims=True)
        W = jax.random.normal(ks[3], (H, D, dh), dtype=jnp.float32) * (1.0 / np.sqrt(D))
        a_src = jax.random.normal(ks[4], (H, dh), dtype=jnp.float32) * (1.0 / np.sqrt(dh))
        a_dst = jax.random.normal(ks[5], (H, dh), dtype=jnp.float32) * (1.0 / np.sqrt(dh))
        beta_tilde = jnp.ones((), dtype=jnp.float32)
        W_out = jax.random.normal(ks[6], (D, D), dtype=jnp.float32) * (1.0 / np.sqrt(D))
        return {'x': x, 'adj': adj, 'prior': prior, 'W': W, 'a_src': a_src, 'a_dst': a_dst, 'beta_tilde': beta_tilde, 'W_out': W_out}
    _L1_gnn_all = _L1_gnn_setup()
    _L1_gnn_in = {k: v for k, v in _L1_gnn_all.items() if k in ('W', 'a_src', 'a_dst', 'beta_tilde', 'W_out')}
    del _L1_gnn_all

    def _L2_gnn_setup():
        import jax, jax.numpy as jnp
        import numpy as np
        EPS = 1e-05

        def _layernorm(x, g, b):
            mu = jnp.mean(x, axis=-1, keepdims=True)
            var = jnp.mean(jnp.square(x - mu), axis=-1, keepdims=True)
            return (x - mu) * jax.lax.rsqrt(var + EPS) * g + b
        key = jax.random.key(seed)
        ks = jax.random.split(key, 8)
        F, N, C, H = (2048, 64, 128, 8)
        x = jax.random.normal(ks[0], (F, N, C), dtype=jnp.float32)
        adj = jax.random.randint(ks[1], (N, N), 0, 2, dtype=jnp.int32)
        adj = jnp.maximum(adj, jnp.eye(N, dtype=jnp.int32))
        s = 1.0 / np.sqrt(C)
        w_qkv = jax.random.normal(ks[2], (C, 3 * C), dtype=jnp.float32) * s
        w1 = jax.random.normal(ks[3], (C, C), dtype=jnp.float32) * s
        b1 = jnp.zeros((C,), dtype=jnp.float32)
        w2 = jax.random.normal(ks[4], (C, C), dtype=jnp.float32) * s
        b2 = jnp.zeros((C,), dtype=jnp.float32)
        ln1_g = jnp.ones((C,), jnp.float32)
        ln1_b = jnp.zeros((C,), jnp.float32)
        ln2_g = jnp.ones((C,), jnp.float32)
        ln2_b = jnp.zeros((C,), jnp.float32)
        return {'x': x, 'adj': adj, 'w_qkv': w_qkv, 'ln1_g': ln1_g, 'ln1_b': ln1_b, 'ln2_g': ln2_g, 'ln2_b': ln2_b, 'w1': w1, 'b1': b1, 'w2': w2, 'b2': b2}
    _L2_gnn_all = _L2_gnn_setup()
    _L2_gnn_in = {k: v for k, v in _L2_gnn_all.items() if k in ('w_qkv', 'ln1_g', 'ln1_b', 'ln2_g', 'ln2_b', 'w1', 'b1', 'w2', 'b2')}
    del _L2_gnn_all

    def _L3_gnn_setup():
        import jax, jax.numpy as jnp
        import numpy as np
        NEG_BIG = -9000000000000000.0
        key = jax.random.key(seed)
        k1, k2, k3, k4 = jax.random.split(key, 4)
        bs, N, Fin, Fout = (8, 1024, 128, 128)
        x = jax.random.normal(k1, (bs, N, Fin), dtype=jnp.float32)
        adj = jax.random.randint(k2, (N, N), 0, 2, dtype=jnp.int32)
        W = jax.random.normal(k3, (Fin, Fout), dtype=jnp.float32) * (1.414 / np.sqrt(Fin))
        a = jax.random.normal(k4, (2 * Fout, 1), dtype=jnp.float32) * 0.1
        return {'x': x, 'adj': adj, 'W': W, 'a': a}
    _L3_gnn_all = _L3_gnn_setup()
    _L3_gnn_in = {k: v for k, v in _L3_gnn_all.items() if k in ('W', 'a')}
    del _L3_gnn_all
    return {'x': x, 'adj': adj, 'L0_gnn_Wq': _L0_gnn_in['Wq'], 'L0_gnn_bq': _L0_gnn_in['bq'], 'L0_gnn_Wk': _L0_gnn_in['Wk'], 'L0_gnn_bk': _L0_gnn_in['bk'], 'L0_gnn_Wv': _L0_gnn_in['Wv'], 'L0_gnn_bv': _L0_gnn_in['bv'], 'L0_gnn_Wo': _L0_gnn_in['Wo'], 'L0_gnn_bo': _L0_gnn_in['bo'], 'L0_gnn_gamma': _L0_gnn_in['gamma'], 'L0_gnn_beta': _L0_gnn_in['beta'], 'L1_gnn_W': _L1_gnn_in['W'], 'L1_gnn_a_src': _L1_gnn_in['a_src'], 'L1_gnn_a_dst': _L1_gnn_in['a_dst'], 'L1_gnn_beta_tilde': _L1_gnn_in['beta_tilde'], 'L1_gnn_W_out': _L1_gnn_in['W_out'], 'L2_gnn_w_qkv': _L2_gnn_in['w_qkv'], 'L2_gnn_ln1_g': _L2_gnn_in['ln1_g'], 'L2_gnn_ln1_b': _L2_gnn_in['ln1_b'], 'L2_gnn_ln2_g': _L2_gnn_in['ln2_g'], 'L2_gnn_ln2_b': _L2_gnn_in['ln2_b'], 'L2_gnn_w1': _L2_gnn_in['w1'], 'L2_gnn_b1': _L2_gnn_in['b1'], 'L2_gnn_w2': _L2_gnn_in['w2'], 'L2_gnn_b2': _L2_gnn_in['b2'], 'L3_gnn_W': _L3_gnn_in['W'], 'L3_gnn_a': _L3_gnn_in['a']}

def reference(x, adj, L0_gnn_Wq, L0_gnn_bq, L0_gnn_Wk, L0_gnn_bk, L0_gnn_Wv, L0_gnn_bv, L0_gnn_Wo, L0_gnn_bo, L0_gnn_gamma, L0_gnn_beta, L1_gnn_W, L1_gnn_a_src, L1_gnn_a_dst, L1_gnn_beta_tilde, L1_gnn_W_out, L2_gnn_w_qkv, L2_gnn_ln1_g, L2_gnn_ln1_b, L2_gnn_ln2_g, L2_gnn_ln2_b, L2_gnn_w1, L2_gnn_b1, L2_gnn_w2, L2_gnn_b2, L3_gnn_W, L3_gnn_a):
    import jax
    import jax.numpy as jnp

    def _L0_gnn_ref(x, adj_matrix, Wq, bq, Wk, bk, Wv, bv, Wo, bo, gamma, beta):
        import jax, jax.numpy as jnp
        import numpy as np
        import math
        CHUNK = 128
        NUM_HEADS = 4
        EPS = 1e-05
        B, N, Fin = x.shape
        H = NUM_HEADS
        Dout = Wq.shape[0]
        Dh = Dout // H
        Nc = N // CHUNK
        q = (x @ Wq.T + bq).reshape(B, N, H, Dh).transpose(0, 2, 1, 3)
        k = (x @ Wk.T + bk).reshape(B, N, H, Dh).transpose(0, 2, 1, 3)
        v = (x @ Wv.T + bv).reshape(B, N, H, Dh).transpose(0, 2, 1, 3)
        kc = k.reshape(B, H, Nc, CHUNK, Dh)
        vc = v.reshape(B, H, Nc, CHUNK, Dh)
        scores = jnp.einsum('bhnd,bhjcd->bhnjc', q, kc) / jnp.sqrt(jnp.asarray(Dh, dtype=q.dtype))
        scores = jnp.clip(scores, -10.0, 10.0)
        mask = adj_matrix.reshape(N, Nc, CHUNK)[None, None]
        scores = jnp.where(mask == 0, jnp.asarray(-10.0, scores.dtype), scores)
        attn = jax.nn.softmax(scores, axis=-1)
        ctx = jnp.einsum('bhnjc,bhjcd->bhnd', attn, vc)
        ctx = ctx.transpose(0, 2, 1, 3).reshape(B, N, Dout)
        out = ctx @ Wo.T + bo
        out = out + x
        mu = jnp.mean(out, axis=-1, keepdims=True)
        var = jnp.mean(jnp.square(out - mu), axis=-1, keepdims=True)
        out = (out - mu) * jax.lax.rsqrt(var + EPS) * gamma + beta
        return out

    def _L1_gnn_ref(x, adj, prior, W, a_src, a_dst, beta_tilde, W_out):
        import jax, jax.numpy as jnp
        import numpy as np
        ALPHA = 0.2
        EPS = 1e-06
        B, N, D = x.shape
        x_proj = jnp.einsum('bnd,hdf->bhnf', x, W)
        e_src = jnp.einsum('bhnf,hf->bhn', x_proj, a_src)
        e_dst = jnp.einsum('bhnf,hf->bhn', x_proj, a_dst)
        e = jax.nn.leaky_relu(e_src[..., :, None] + e_dst[..., None, :], ALPHA)
        beta = jax.nn.softplus(beta_tilde)
        e = e + (beta * jnp.log(prior + EPS))[:, None, :, :]
        neg_inf = jnp.finfo(e.dtype).min
        e = jnp.where(adj[None, None, :, :] > 0, e, neg_inf)
        attn = jax.nn.softmax(e, axis=-1)
        h = jnp.einsum('bhij,bhjf->bhif', attn, x_proj)
        h = h.transpose(0, 2, 1, 3).reshape(B, N, D)
        return h @ W_out.T

    def _L2_gnn_ref(x, adj, w_qkv, ln1_g, ln1_b, ln2_g, ln2_b, w1, b1, w2, b2):
        import jax, jax.numpy as jnp
        import numpy as np
        EPS = 1e-05

        def _layernorm(x, g, b):
            mu = jnp.mean(x, axis=-1, keepdims=True)
            var = jnp.mean(jnp.square(x - mu), axis=-1, keepdims=True)
            return (x - mu) * jax.lax.rsqrt(var + EPS) * g + b
        F, N, C = x.shape
        H = 8
        D = C // H
        qkv = jnp.einsum('fnc,ck->fnk', x, w_qkv)
        q, k, v = jnp.split(qkv, 3, axis=-1)
        q = q.reshape(F, N, H, D)
        k = k.reshape(F, N, H, D)
        v = v.reshape(F, N, H, D)
        scores = jnp.einsum('fnhd,fmhd->fhnm', q, k) / jnp.sqrt(jnp.asarray(D, x.dtype))
        mask = (adj > 0)[None, None, :, :]
        scores = jnp.where(mask, scores, jnp.asarray(-1000000000.0, x.dtype))
        attn = jax.nn.softmax(scores, axis=-1)
        t = jnp.einsum('fhnm,fmhd->fnhd', attn, v).reshape(F, N, C)
        x = _layernorm(x + t, ln1_g, ln1_b)
        h = jax.nn.relu(jnp.einsum('fnc,cd->fnd', x, w1) + b1)
        f_out = jnp.einsum('fnd,dc->fnc', h, w2) + b2
        x = _layernorm(x + f_out, ln2_g, ln2_b)
        return x

    def _L3_gnn_ref(x, adj, W, a):
        import jax, jax.numpy as jnp
        import numpy as np
        NEG_BIG = -9000000000000000.0
        alpha = 0.2
        h = jnp.matmul(x, W)
        Fout = h.shape[-1]
        a1, a2 = (a[:Fout, 0], a[Fout:, 0])
        s1 = jnp.einsum('bnf,f->bn', h, a1)
        s2 = jnp.einsum('bnf,f->bn', h, a2)
        e = jax.nn.leaky_relu(s1[:, :, None] + s2[:, None, :], negative_slope=alpha)
        attention = jnp.where(adj[None, :, :] > 0, e, NEG_BIG)
        attention = jax.nn.softmax(attention, axis=-1)
        h_prime = jnp.matmul(attention, h)
        return jax.nn.elu(h_prime)
    h = jnp.maximum(_layernorm(x, axis=-1), 0.0)
    x = x + _L0_gnn_ref(h, adj, L0_gnn_Wq, L0_gnn_bq, L0_gnn_Wk, L0_gnn_bk, L0_gnn_Wv, L0_gnn_bv, L0_gnn_Wo, L0_gnn_bo, L0_gnn_gamma, L0_gnn_beta)
    h = jnp.maximum(_layernorm(x, axis=-1), 0.0)
    x = x + _L1_gnn_ref(h, adj, adj[None], L1_gnn_W, L1_gnn_a_src, L1_gnn_a_dst, L1_gnn_beta_tilde, L1_gnn_W_out)
    h = jnp.maximum(_layernorm(x, axis=-1), 0.0)
    x = x + _L2_gnn_ref(h, adj, L2_gnn_w_qkv, L2_gnn_ln1_g, L2_gnn_ln1_b, L2_gnn_ln2_g, L2_gnn_ln2_b, L2_gnn_w1, L2_gnn_b1, L2_gnn_w2, L2_gnn_b2)
    h = jnp.maximum(_layernorm(x, axis=-1), 0.0)
    x = x + _L3_gnn_ref(h, adj, L3_gnn_W, L3_gnn_a)
    return x

_drawn_inputs = setup_inputs


def setup_inputs(seed=0):
    import zlib

    import numpy as np

    out = dict(_drawn_inputs(seed))
    spreads = {'L0_gnn_bq': (0.0, 2.0),
     'L0_gnn_bk': (0.0, 2.0),
     'L0_gnn_bv': (0.0, 0.1),
     'L0_gnn_bo': (0.0, 0.394),
     'L0_gnn_gamma': (1.0, 0.2),
     'L0_gnn_beta': (0.0, 0.1),
     'L2_gnn_ln1_g': (1.0, 0.2),
     'L2_gnn_ln1_b': (0.0, 0.1),
     'L2_gnn_ln2_g': (1.0, 0.2),
     'L2_gnn_ln2_b': (0.0, 0.1),
     'L2_gnn_b1': (0.0, 0.331),
     'L2_gnn_b2': (0.0, 0.1)}
    factors = {'L1_gnn_a_src': 2.83}
    for name, (base, spread) in spreads.items():
        noise = np.random.default_rng([zlib.crc32(name.encode()), seed]).standard_normal(out[name].shape)
        drawn = base * np.exp(spread * noise) if base else spread * noise
        out[name] = jnp.asarray(drawn.astype(out[name].dtype))
    for name, factor in factors.items():
        out[name] = (out[name] * factor).astype(out[name].dtype)
    return out
```

```python
from contextlib import ExitStack

import concourse.bass as bass
from concourse import mybir

F32 = mybir.dt.float32
BF16 = mybir.dt.bfloat16
I32 = mybir.dt.int32
ALU = mybir.AluOpType
ACT = mybir.ActivationFunctionType
AX = mybir.AxisListType

P = 128
NT = 8
N = P * NT
D = 128
HALF = 512
H0, DH0 = 4, 32
H1, DH1 = 8, 16
BIG = float(2.0 ** 100)
EPS_LN = 1e-5
EPS_PRIOR = 1e-6
SLOPE = 0.2
CLIP = 10.0

TERMS0 = [[(0, 0), (0, 1), (1, 0), (0, 2)], [(2, 0), (1, 1), (1, 2)]]
TERMS2 = [(0, 0), (0, 1), (1, 0), (0, 2), (2, 0), (1, 1)]
K0 = [len(t) * DH0 for t in TERMS0]
K2 = len(TERMS2) * DH1
ACT_TILES = 6


class Signal:

    def __init__(self, nc, ctx, name, per_batch, before=0):
        self.name, self.per, self.given, self.before = name, per_batch, 0, before
        self.sem = ctx.enter_context(nc.semaphore(name))

    def at(self, b, count):
        return b * self.per + (count + self.before)

    def by(self, ins, n=1):
        self.given += n
        ins.then_inc(self.sem, n)
        return ins


def program(nc, x, adj, w, out, B):
    with ExitStack() as ctx:
        def sb(name, shape, dt=F32):
            return ctx.enter_context(nc.sbuf_tensor(name, shape, dt))

        def signal(name, per_batch, before=0):
            s = Signal(nc, ctx, name, per_batch, before)
            signals.append(s)
            return s

        signals = []
        ps = ctx.enter_context(nc.psum_tensor("ps", [P, 8, HALF], F32))

        ident = sb("ident", [P, P])
        ident_b = sb("ident_b", [P, P], BF16)
        neg_ident_b = sb("neg_ident_b", [P, P], BF16)
        ones = sb("ones", [P, H1 * (DH1 + 1)])
        ones_b = sb("ones_b", [1, N], BF16)
        tick = sb("tick", [1, 4])
        neg_half = sb("neg_half", [P, NT])
        mask_t = sb("mask_t", [P, NT, N], BF16)
        limit_t = sb("limit_t", [P, NT, N], BF16)
        block_t = sb("block_t", [P, NT, N], BF16)
        block_n = sb("block_n", [P, NT, N], BF16)
        empty = sb("empty", [P, NT])
        wT = sb("wT", [P, 5, D])
        bcol = sb("bcol", [P, 4])
        brow = sb("brow", [P, 9, D])
        w1cat = sb("w1cat", [P, D + 2 * H1])
        w3cat = sb("w3cat", [P, D + 2])
        wqkv = sb("wqkv", [P, 3 * D])
        ffn1 = sb("ffn1", [P, D])
        ffn2 = sb("ffn2", [P, D])
        BV, BO, GAMMA, BETA, G1, BE1, G2, BE2, B2 = range(9)

        xin = sb("xin", [P, NT, D])
        xr = sb("xr", [P, NT, D])
        hn = sb("hn", [P, NT, D])
        hT = sb("hT", [P, N])
        bufc = sb("bufc", [P, NT, D])
        bufd = sb("bufd", [P, NT, D])
        parts = sb("parts", [P, 2, 3, N], BF16)
        arena = sb("arena", [P, 2, NT * HALF])
        maps = sb("maps", [P, NT, N])
        v2 = sb("v2", [P, NT, H1, 32])
        v1 = sb("v1", [P, NT, H1, DH1 + 1])
        v3 = sb("v3", [P, NT, 1, D + 1])
        gsum = sb("gsum", [P, NT, H1, DH1 + 1])
        csum = sb("csum", [P, H1 * (DH1 + 1)])
        stats = sb("stats", [P, NT, 6])
        mv = sb("mv", [P, NT, 2])
        rstd = sb("rstd", [P, NT])
        shift = sb("shift", [P, NT])
        sd = sb("sd", [P, NT, 2 * H1])
        dmx = sb("dmx", [P, H1])
        dmc = sb("dmc", [P, 1])
        dmdiag = sb("dmdiag", [P, H1])
        dmax = sb("dmax", [P, H1])
        arg = sb("arg", [P, 4, NT, H1])
        ew = sb("ew", [P, 4, NT, H1])
        tm = sb("tm", [P, 2, NT, H1])
        rden = sb("rden", [P, NT * H1])
        msplit = sb("msplit", [P, 2, NT, 2])
        mtop = sb("mtop", [P, 2, NT])
        mneg = sb("mneg", [P, 2, NT], BF16)
        junk = sb("junk", [P, 3, HALF], BF16)

        flat = lambda t: t.rearrange("p t f -> p (t f)")
        stq = arena[:, 0, :].bitcast(BF16).rearrange("p (h n) -> p h n", n=N)
        stk = arena[:, 1, :].bitcast(BF16).rearrange("p (h n) -> p h n", n=N)
        step = maps[:, 0:4, :].rearrange("p t n -> p (t n)").bitcast(BF16).rearrange("p (t n) -> p t n", n=N)
        rest = maps[:, 4:8, :].rearrange("p t n -> p (t n)").bitcast(BF16).rearrange("p (t n) -> p t n", n=N)
        sbc = maps[:, 4:6, :]
        resid = maps[:, 0:2, :]
        ctx2 = maps[:, 4:8, :].rearrange("p t (s n) -> p (t s) n", n=HALF)
        sign = parts[:, :, :, :].rearrange("p a b n -> p (a b) n")[:, 0:4, :]
        F1 = DH1 + 1
        F3 = D + 1
        kview = arena[:, 1, :].bitcast(BF16)
        r1 = kview[:, 0:NT * H1 * 6 * F1].rearrange("p (t h s r f) -> p t h s r f", h=H1, s=2, r=3, f=F1)
        r3 = kview[:, 0:NT * 6 * F3].rearrange("p (t h s r f) -> p t h s r f", h=1, s=2, r=3, f=F3)

        def qview(at, nh, f):
            return arena[:, 0, at:at + NT * nh * f].rearrange("p (t h f) -> p t h f", h=nh, f=f)

        def gat_views(nh, f):
            n = NT * nh * f
            return (qview(0, nh, f), qview(n, nh, f),
                    arena[:, 0, 0:2 * n].rearrange("p (t h s f) -> p t h s f", h=nh, s=2, f=f))

        v0 = gsum[:, :, :, :].rearrange("p t h f -> p (t h f)")[:, 0:NT * D].rearrange(
            "p (t h f) -> p t h f", h=H0, f=DH0)
        inv0 = flat(bufd[:, :, :])

        x_landed = signal("x_landed", 16)
        x_freed = signal("x_freed", 1, before=1)
        x_done = signal("x_done", 1)
        x_stored = signal("x_stored", 16, before=1)
        ln_var = signal("ln_var", 7)
        ln_rstd = signal("ln_rstd", 7)
        ln_coef = signal("ln_coef", 7)
        h_tile = signal("h_tile", 4 * NT)
        normed = signal("normed", 3)
        turned = signal("turned", 2 * 6 + 2 * H1 // 2)
        actT = signal("actT", 2 * 6)
        qk_ps = signal("qk_ps", 4)
        v_ps = signal("v_ps", 2)
        part_h = signal("part_h", 4)
        parts_ready = signal("parts_ready", 4)
        v_ready = signal("v_ready", 2)
        stack = [signal(f"stack{h}", 16 * (2 * sum(map(len, TERMS0)) * (h < H0) + 2 * len(TERMS2)))
                 for h in range(H1)]
        s0_ready = signal("s0_ready", H0 * NT)
        clip_ready = signal("clip_ready", H0 * NT)
        p0_ready = signal("p0_ready", H0 * NT)
        pv0 = signal("pv0", 2 * NT)
        share0 = signal("share0", 2 * NT)
        ctx0 = signal("ctx0", 2 * (NT - 1))
        lin_ps = signal("lin_ps", 6)
        lin_out = signal("lin_out", 2)
        top1 = signal("top1", 2)
        top1T = signal("top1T", 2)
        top_diag = signal("top_diag", 2)
        top_ps = signal("top_ps", 2)
        args_ready = signal("args_ready", 2)
        weights = signal("weights", 2)
        rows_ps = signal("rows_ps", H1 + 1)
        rows_out = signal("rows_out", H1 + 1)
        sign_ready = signal("sign_ready", ACT_TILES * (H1 + 1))
        step_ready = signal("step_ready", NT * (H1 + 1))
        step_used = signal("step_used", NT * H1)
        rest_ready = signal("rest_ready", NT)
        ra_ready = signal("ra_ready", 2)
        rb_ready = signal("rb_ready", 2)
        csum_ps = signal("csum_ps", 2)
        csum_out = signal("csum_out", 2)
        g_ps = signal("g_ps", NT)
        g_out = signal("g_out", NT)
        t_out = signal("t_out", H1)
        t3_ps = signal("t3_ps", NT)
        t3_out = signal("t3_out", NT)
        hn1_ready = signal("hn1_ready", 1)
        nat_ps = signal("nat_ps", H1 * NT * 2)
        nat_used = signal("nat_used", H1 * NT * 2)
        mneg_ready = signal("mneg_ready", H1)
        mrow_ps = signal("mrow_ps", H1)
        mrow_ready = signal("mrow_ready", H1)
        ones_row = signal("ones_row", 16)
        s2_ready = signal("s2_ready", H1 * NT)
        p2_ready = signal("p2_ready", H1 * NT)
        pv2 = signal("pv2", H1 * NT // 2)
        ctx2_out = signal("ctx2_out", H1)
        ctx2_nat = signal("ctx2_nat", H1 // 2)
        x1_ready = signal("x1_ready", 1)
        elu_ready = signal("elu_ready", 1)
        z_out = signal("z_out", 2)
        dve = signal("dve_chain", DVE_CHAIN)
        pool = signal("pool_chain", POOL_CHAIN)
        act_free = signal("act_chain", ACT_CHAIN)
        loaded = signal("loaded", 0)
        set_pool = signal("set_pool", 0)
        set_dve = signal("set_dve", 0)
        set_pe = signal("set_pe", 0)
        set_act = signal("set_act", 0)

        block = ctx.enter_context(nc.Block())

        carried = [0]

        def carry(ve):
            carried[0] += 1
            ve.memset(tick[0:1, carried[0] % 4:carried[0] % 4 + 1], 0.0)

        x_v = x.rearrange("b (t p) f -> b p t f", p=P)
        out_v = out.rearrange("b (t p) f -> b p t f", p=P)
        adj_i = maps[:, :, :].bitcast(I32)
        nat01 = arena[:, :, :].rearrange("p a n -> p (a n)").bitcast(BF16)[:, 0:NT * N].rearrange(
            "p (t n) -> p t n", n=N)
        raw_w = bufc[:, 0:5, :]
        a_row = bufd[:, 0:4, :]
        a_tmp = hn[:, :, :]
        beta_c = shift[:, 0:1]

        LOADS = [
            (adj_i[:, :, :], adj.rearrange("(t p) n -> p t n", p=P)),
            (raw_w[:, 0, :], w["L0_gnn_Wq"]), (raw_w[:, 1, :], w["L0_gnn_Wk"]),
            (raw_w[:, 2, :], w["L0_gnn_Wv"]), (raw_w[:, 3, :], w["L0_gnn_Wo"]),
            (raw_w[:, 4, :], w["L1_gnn_W_out"]),
            (w1cat[:, 0:D].rearrange("p (h f) -> p h f", f=DH1), w["L1_gnn_W"].rearrange("h d f -> d h f")),
            (w3cat[:, 0:D], w["L3_gnn_W"]), (wqkv[:, :], w["L2_gnn_w_qkv"]),
            (ffn1[:, :], w["L2_gnn_w1"]), (ffn2[:, :], w["L2_gnn_w2"]),
            (bcol[:, 0:1], w["L0_gnn_bq"].rearrange("(p a) -> p a", a=1)),
            (bcol[:, 1:2], w["L0_gnn_bk"].rearrange("(p a) -> p a", a=1)),
            (bcol[:, 2:3], w["L2_gnn_b1"].rearrange("(p a) -> p a", a=1)),
            (a_row[:, 0, :], w["L1_gnn_a_src"].rearrange("h f -> (h f)").partition_broadcast(P)),
            (a_row[:, 1, :], w["L1_gnn_a_dst"].rearrange("h f -> (h f)").partition_broadcast(P)),
            (a_row[:, 2:4, :].rearrange("p a f -> p (a f)"),
             w["L3_gnn_a"].rearrange("n a -> (n a)").partition_broadcast(P)),
            (beta_c, w["L1_gnn_beta_tilde"].partition_broadcast(P)),
        ] + [(brow[:, n, :], w[name].partition_broadcast(P)) for n, name in enumerate(
            ["L0_gnn_bv", "L0_gnn_bo", "L0_gnn_gamma", "L0_gnn_beta", "L2_gnn_ln1_g", "L2_gnn_ln1_b",
             "L2_gnn_ln2_g", "L2_gnn_ln2_b", "L2_gnn_b2"])]

        def copy_stack(sp, h, term, rows, qp, kp, base, slot):
            for u, (st, part) in enumerate(((stq, qp), (stk, kp))):
                dma = sp.dma_start(st[term * rows:(term + 1) * rows, slot, :],
                                   parts[base:base + rows, u, part, :])
                stack[h].by(dma, 16)

        @block.sync
        def _(sp):
            for dst, src in LOADS:
                loaded.by(sp.dma_start(dst, src), 16)
            sp.wait_ge(set_pool.sem, 9)
            with sp.Fori(0, B) as b:
                sp.wait_ge(x_freed.sem, x_freed.at(b, 0))
                x_landed.by(sp.dma_start(xin[:, :, :], x_v[b]), 16)
                sp.wait_ge(parts_ready.sem, parts_ready.at(b, 2))
                for h in range(H0):
                    for s, terms in enumerate(TERMS0):
                        for t, (qp, kp) in enumerate(terms):
                            copy_stack(sp, h, t, DH0, qp, kp, h * DH0, 2 * h + s)
                sp.wait_ge(parts_ready.sem, parts_ready.at(b, 4))
                ones_row.by(sp.dma_start(stk[K2:K2 + 1, :, :],
                                         ones_b[0:1, :].unsqueeze(1).broadcast_to([1, H1, N])), 16)
                for h in range(H1):
                    for t, (qp, kp) in enumerate(TERMS2):
                        copy_stack(sp, h, t, DH1, qp, kp, h * DH1, h)
                sp.wait_ge(x_done.sem, x_done.at(b, 1))
                x_stored.by(sp.dma_start(out_v[b], xr[:, :, :]), 16)
            sp.wait_ge(x_stored.sem, x_stored.at(B, 0))

        @block.gpsimd
        def _(gp):
            set_pool.by(gp.memset(ident[:, :], 0.0))
            set_pool.by(gp.memset(ones[:, :], 1.0))
            set_pool.by(gp.memset(ones_b[:, :], 1.0))
            set_pool.by(gp.memset(neg_half[:, :], -0.5))
            set_pool.by(gp.memset(v1[:, :, :, DH1:F1], 1.0))
            set_pool.by(gp.memset(v3[:, :, :, D:F3], 1.0))
            set_pool.by(gp.memset(v2[:, :, :, DH1:F1], 1.0))
            set_pool.by(gp.memset(v2[:, :, :, F1:32], 0.0))
            gp.wait_ge(set_pool.sem, 8)
            set_pool.by(gp.affine_select(out=ident[:, :], in_=ident[:, :], compare_op=ALU.not_equal, fill=1.0,
                                         base=0, pattern=[[-1, P]], channel_multiplier=1))
            chain = [0]
            with gp.Fori(0, B) as b:
                def link(ins):
                    chain[0] += 1
                    pool.by(ins)
                    gp.wait_ge(pool.sem, pool.at(b, chain[0]))

                def inv_root(k):
                    gp.wait_ge(ln_var.sem, ln_var.at(b, k + 1))
                    ln_rstd.by(gp.tensor_tensor(rstd[:, :], mv[:, :, 1], neg_half[:, :], ALU.pow))

                def split_low(nh, f, r, src, which):
                    gp.wait_ge(weights.sem, weights.at(b, which + 1))
                    _, vb, _ = gat_views(nh, f)
                    wb = ew[:, 3, :, 0:nh].unsqueeze(3).broadcast_to([P, NT, nh, f])
                    link(gp.tensor_tensor(vb, src, wb, ALU.mult))
                    one = ones[:, 0:nh * f].rearrange("p (h f) -> p h f", h=nh).unsqueeze(1).broadcast_to(
                        [P, NT, nh, f])
                    link(gp.tensor_tensor(r[:, :, :, 1, 0, :], vb, one, ALU.mult))
                    link(gp.tensor_tensor(vb, vb, r[:, :, :, 1, 0, :], ALU.subtract))
                    link(gp.tensor_tensor(r[:, :, :, 1, 1, :], vb, one, ALU.mult))
                    rb_ready.by(gp.tensor_tensor(r[:, :, :, 1, 2, :], vb, r[:, :, :, 1, 1, :], ALU.subtract))

                inv_root(0)
                for m in range(2, 2 * NT):
                    gp.wait_ge(share0.sem, share0.at(b, m + 1))
                    if m >= 4:
                        gp.wait_ge(ctx0.sem, ctx0.at(b, m - 3))
                    half = flat(bufc[:, :, :])[:, (m % 2) * HALF:(m % 2 + 1) * HALF]
                    ctx0.by(gp.tensor_tensor(half, half, hT[:, (m % 2) * HALF:(m % 2 + 1) * HALF], ALU.add))
                inv_root(1)
                inv_root(2)
                split_low(H1, F1, r1, v1[:, :, :, :], 0)
                inv_root(3)
                inv_root(4)
                inv_root(5)
                inv_root(6)
                split_low(1, F3, r3, v3[:, :, :, :], 1)
            assert chain[0] == pool.per, ("POOL_CHAIN", chain[0])

        @block.scalar
        def _(act):
            act.wait_ge(loaded.sem, 16 * len(LOADS))
            set_act.by(act.activation(tm[:, 0, 0, 0:1], beta_c, ACT.Abs))
            act.wait_ge(set_act.sem, 1)
            set_act.by(act.activation(tm[:, 0, 1, 0:1], tm[:, 0, 0, 0:1], ACT.Exp, scale=-1.0))
            act.wait_ge(set_act.sem, 2)
            act.wait_ge(set_dve.sem, 1)
            act.wait_ge(set_pool.sem, 9)
            set_act.by(act.activation(tm[:, 0, 2, 0:1], tm[:, 0, 1, 0:1], ACT.Ln, bias=ones[:, 0:1]))
            set_act.by(act.activation(tm[:, 0, 3, 0:1], tm[:, 0, 4, 0:1], ACT.Ln))
            chain = [0]
            with act.Fori(0, B) as b:
                def link(ins):
                    chain[0] += 1
                    act_free.by(ins)
                    act.wait_ge(act_free.sem, act_free.at(b, chain[0]))

                def norm_relu(src, k, m):
                    act.wait_ge(ln_coef.sem, ln_coef.at(b, k + 1))
                    for t in range(NT):
                        h_tile.by(act.activation(hn[:, t, :], src[:, t, :], ACT.Relu, bias=shift[:, t:t + 1],
                                                 scale=rstd[:, t:t + 1]))

                def norm_plain(src, dst, k, m):
                    act.wait_ge(ln_coef.sem, ln_coef.at(b, k + 1))
                    for t in range(NT):
                        ins = act.activation(dst[:, t, :], src[:, t, :], ACT.Identity, bias=shift[:, t:t + 1],
                                             scale=rstd[:, t:t + 1])
                    normed.by(ins)

                def turn_out(dst, event, m):
                    for half in range(2):
                        act.wait_ge(turned.sem, turned.at(b, event + half + 1))
                        actT.by(act.copy(dst[:, half * HALF:(half + 1) * HALF], ps[:, 6 + half, :]))

                def high_parts(layer):
                    for u in range(2):
                        act.wait_ge(qk_ps.sem, qk_ps.at(b, 2 * layer + u + 1))
                        if layer == 0:
                            ins = act.activation(parts[:, u, 0, :].rearrange("p (a n) -> p a n", a=2),
                                                 ps[:, 2 * u:2 * u + 2, :], ACT.Identity, bias=bcol[:, u:u + 1])
                        else:
                            ins = act.copy(parts[:, u, 0, :].rearrange("p (a n) -> p a n", a=2),
                                           ps[:, 2 * u:2 * u + 2, :])
                        part_h.by(ins)

                def rows(n, bank, dst):
                    act.wait_ge(rows_ps.sem, rows_ps.at(b, n + 1))
                    if 2 <= n < H1:
                        act.wait_ge(step_ready.sem, step_ready.at(b, NT * (n - 1)))
                    rows_out.by(act.copy(dst.rearrange("p (a n) -> p a n", a=2), ps[:, bank:bank + 2, :]))

                def signs(n, jts, src, nh, h):
                    act.wait_ge(rows_out.sem, rows_out.at(b, n + 1))
                    for jt in jts:
                        k = n * ACT_TILES + jt
                        if k >= 4:
                            old = k - 4
                            act.wait_ge(step_ready.sem, step_ready.at(
                                b, old // ACT_TILES * NT + old % ACT_TILES + 1))
                        sign_ready.by(act.activation(sign[:, k % 4, :], src, ACT.Sign,
                                                     bias=sd[:, jt, nh + h:nh + h + 1]))

                norm_relu(xin, 0, 0)
                turn_out(hT, 0, 0)
                high_parts(0)
                for n in range(H0 * NT):
                    act.wait_ge(clip_ready.sem, clip_ready.at(b, n + 1))
                    p0_ready.by(act.activation(maps[:, n % 8, :], maps[:, n % 8, :], ACT.Exp))
                norm_plain(bufc, bufd, 1, 0)
                norm_relu(xr, 2, 1)
                turn_out(hT, 2, 1)
                act.wait_ge(lin_out.sem, lin_out.at(b, 1))
                rows(0, 0, sbc[:, 0, :])
                signs(0, range(4), sbc[:, 0, :], H1, 0)
                act.wait_ge(args_ready.sem, args_ready.at(b, 1))
                weights.by(act.activation(ew[:, :, :, :], arg[:, :, :, :], ACT.Exp))
                signs(0, range(4, ACT_TILES), sbc[:, 0, :], H1, 0)
                for h in range(1, H1):
                    rows(h, 2 * (h % 2), sbc[:, h % 2, :])
                    signs(h, range(ACT_TILES), sbc[:, h % 2, :], H1, h)
                turn_out(flat(bufd[:, :, :]), 4, 2)
                norm_relu(xr, 3, 2)
                turn_out(hT, 6, 3)
                high_parts(1)
                for h in range(H1):
                    def max_row(h):
                        act.wait_ge(mrow_ps.sem, mrow_ps.at(b, h + 1))
                        mrow_ready.by(act.copy(stq[K2:K2 + 1, h, :].rearrange("p (a n) -> p a n", a=2),
                                               ps[K2:K2 + 1, 6:8, :]))

                    if h == 0:
                        max_row(0)
                    for jt in range(NT):
                        n = h * NT + jt
                        act.wait_ge(s2_ready.sem, s2_ready.at(b, n + 1))
                        if n >= 4:
                            act.wait_ge(pv2.sem, pv2.at(b, (n - 4) // 2 + 1))
                        p2_ready.by(act.activation(maps[:, n % 4, :].rearrange("p (a n) -> p a n", a=2),
                                                   ps[:, 2 * (n % 2):2 * (n % 2) + 2, :], ACT.Exp))
                        if jt == 1 and h > 0:
                            act.wait_ge(pv2.sem, pv2.at(b, NT // 2 * h))
                            ctx2_out.by(act.copy(ctx2[:, h - 1, :], ps[:, 4 + (h - 1) % 2, :]))
                        if jt == NT - 2 and h + 1 < H1:
                            max_row(h + 1)
                act.wait_ge(pv2.sem, pv2.at(b, NT // 2 * H1))
                ctx2_out.by(act.copy(ctx2[:, H1 - 1, :], ps[:, 4 + (H1 - 1) % 2, :]))
                norm_plain(bufc, bufd, 4, 1)
                turn_out(hT, 8 + H1, 4)
                act.wait_ge(lin_ps.sem, lin_ps.at(b, 4))
                for half in range(2):
                    z_out.by(act.activation(flat(bufd[:, 4 * half:4 * half + 4, :]), ps[:, half, :], ACT.Relu,
                                            bias=bcol[:, 2:3]))
                norm_plain(bufc, bufd, 5, 2)
                norm_relu(xr, 6, 3)
                turn_out(hT, 10 + H1, 5)
                act.wait_ge(lin_out.sem, lin_out.at(b, 2))
                rows(H1, 0, flat(bufd[:, :, :]))
                signs(H1, range(4), flat(bufd[:, :, :]), 1, 0)
                act.wait_ge(args_ready.sem, args_ready.at(b, 2))
                weights.by(act.activation(ew[:, :, :, 0:1], arg[:, :, :, 0:1], ACT.Exp))
                signs(H1, range(4, ACT_TILES), flat(bufd[:, :, :]), 1, 0)
                act.wait_ge(elu_ready.sem, elu_ready.at(b, 1))
                link(act.activation(hn[:, :, :], bufc[:, :, :], ACT.Exp))
            assert chain[0] == act_free.per, ("ACT_CHAIN", chain[0])

        @block.vector
        def _(ve):
            chain = [0]

            ve.wait_ge(loaded.sem, 16 * len(LOADS))
            ve.memset(tm[:, 0, 4, 0:1], 1.0 + EPS_PRIOR).then_inc(set_dve.sem, 1)
            ve.wait_ge(set_pool.sem, 9)
            done = [1]

            def seq(ins):
                done[0] += 1
                ins.then_inc(set_dve.sem, 1)
                ve.wait_ge(set_dve.sem, done[0])

            seq(ve.tensor_copy(ident_b[:, :], ident[:, :]))
            seq(ve.tensor_scalar(neg_ident_b[:, :], ident[:, :], -1.0, None, ALU.mult))
            seq(ve.tensor_scalar(nat01[:, :, :], adj_i[:, :, :], 0.0, None, ALU.is_gt))
            seq(ve.tensor_reduce(rden[:, 0:NT], nat01[:, :, :], AX.X, ALU.add))
            seq(ve.tensor_scalar(empty[:, :], rden[:, 0:NT], 0.0, None, ALU.is_equal))
            seq(ve.tensor_scalar(block_n[:, :, :], nat01[:, :, :], -1.0, BIG, ALU.add, ALU.mult))
            NAT_SET = done[0]
            for n, (wc, nh, f) in enumerate(((w1cat, H1, DH1), (w1cat, H1, DH1), (w3cat, 1, D), (w3cat, 1, D))):
                seq(ve.tensor_tensor(a_tmp[:, n, :], wc[:, 0:D], a_row[:, n, :], ALU.mult))
                at = D + (n % 2) * nh
                seq(ve.tensor_reduce(wc[:, at:at + nh], a_tmp[:, n, :].rearrange("p (h f) -> p h f", f=f),
                                     AX.X, ALU.add))
            seq(ve.tensor_scalar(wqkv[:, 0:D], wqkv[:, 0:D], DH1 ** -0.5, None, ALU.mult))
            seq(ve.tensor_scalar(bcol[:, 0:1], bcol[:, 0:1], DH0 ** -0.5, None, ALU.mult))
            ve.wait_ge(set_act.sem, 4)
            seq(ve.tensor_scalar(tm[:, 0, 5, 0:1], beta_c, 0.0, None, ALU.max))
            seq(ve.tensor_tensor(tm[:, 0, 6, 0:1], tm[:, 0, 5, 0:1], tm[:, 0, 2, 0:1], ALU.add))
            seq(ve.tensor_tensor(bcol[:, 3:4], tm[:, 0, 6, 0:1], tm[:, 0, 3, 0:1], ALU.mult))
            ve.wait_ge(set_pe.sem, 1)
            seq(ve.tensor_scalar(wT[:, 0, :], ps[:, 0, 0:D], DH0 ** -0.5, None, ALU.mult))
            seq(ve.tensor_copy(wT[:, 1:4, :], ps[:, 0, D:4 * D].rearrange("p (a f) -> p a f", a=3)))
            seq(ve.tensor_copy(wT[:, 4, :], ps[:, 1, 0:D]))
            for jt in range(NT):
                ve.wait_ge(set_pe.sem, 2 + jt)
                seq(ve.tensor_copy(mask_t[:, jt, :], ps[:, 2 + jt % 2, :].bitcast(BF16)))
            TURN_SET = done[0]
            seq(ve.tensor_scalar(limit_t[:, :, :], mask_t[:, :, :], 2 * CLIP, -CLIP, ALU.mult, ALU.add))
            seq(ve.tensor_scalar(block_t[:, :, :], mask_t[:, :, :], -BIG, BIG, ALU.mult, ALU.add))
            setup_marks.update(nat=NAT_SET, turn=TURN_SET, end=done[0])

            ve.memset(tick[0:1, 0:1], 0.0).then_inc(x_freed.sem, 1)
            ve.memset(tick[0:1, 2:3], 0.0).then_inc(x_stored.sem, 1)

            with ve.Fori(0, B) as b:
                def link(ins):
                    chain[0] += 1
                    dve.by(ins)
                    ve.wait_ge(dve.sem, dve.at(b, chain[0]))

                def ln(src, k):
                    for t in range(NT):
                        ins = ve.bn_stats(stats[:, t, :], src[:, t, :])
                    link(ins)
                    carry(ve)
                    for t in range(NT):
                        ins = ve.bn_aggr(mv[:, t, :], stats[:, t, :])
                    link(ins)
                    ln_var.by(ve.tensor_scalar(mv[:, :, 1], mv[:, :, 1], EPS_LN, None, ALU.add))
                    ve.wait_ge(ln_rstd.sem, ln_rstd.at(b, k + 1))
                    ln_coef.by(ve.scalar_tensor_tensor(shift[:, :], mv[:, :, 0], -1.0, rstd[:, :],
                                                       ALU.mult, ALU.mult))

                def row(v):
                    return brow[:, v:v + 1, :].broadcast_to([P, NT, D])

                def low_parts(layer):
                    for u in range(2):
                        ve.wait_ge(part_h.sem, part_h.at(b, 2 * layer + u + 1))
                        acc = ps[:, 2 * u:2 * u + 2, :].rearrange("p a n -> p (a n)")
                        if layer == 0:
                            link(ve.scalar_tensor_tensor(resid[:, u, :], acc, bcol[:, u:u + 1],
                                                         parts[:, u, 0, :], ALU.add, ALU.subtract))
                        else:
                            link(ve.tensor_tensor(resid[:, u, :], acc, parts[:, u, 0, :], ALU.subtract))
                        link(ve.tensor_copy(parts[:, u, 1, :], resid[:, u, :]))
                        parts_ready.by(ve.tensor_tensor(parts[:, u, 2, :], resid[:, u, :], parts[:, u, 1, :],
                                                        ALU.subtract))

                def gat_out_of_psum(nh, f, v, cat):
                    for g in range(3):
                        k = min(3, NT - 3 * g)
                        acc = ps[:, g, 0:k * cat].rearrange("p (t c) -> p t c", c=cat)
                        ve.tensor_copy(v[:, 3 * g:3 * g + k, :, 0:f - 1],
                                       acc[:, :, 0:D].rearrange("p t (h f) -> p t h f", h=nh))
                        ins = ve.tensor_copy(sd[:, 3 * g:3 * g + k, 0:2 * nh], acc[:, :, D:D + 2 * nh])
                    lin_out.by(ins)

                def gat_weights(nh, which):
                    s, d = sd[:, :, 0:nh], sd[:, :, nh:2 * nh]
                    ve.wait_ge(lin_out.sem, lin_out.at(b, which + 1))
                    top1.by(ve.tensor_reduce(dmx[:, 0:nh], d.rearrange("p t h -> p h t"), AX.X, ALU.max))
                    ve.wait_ge(top1T.sem, top1T.at(b, which + 1))
                    link(ve.tensor_reduce(dmc[0:nh, :], ps[0:nh, 6, 0:P], AX.X, ALU.max))
                    top_diag.by(ve.tensor_scalar(dmdiag[0:nh, 0:nh], ident[0:nh, 0:nh], dmc[0:nh, 0:1], None,
                                                 ALU.mult))
                    ve.wait_ge(top_ps.sem, top_ps.at(b, which + 1))
                    link(ve.tensor_copy(dmax[:, 0:nh], ps[:, 7, 0:nh]))
                    top = dmax[:, 0:nh].unsqueeze(1).broadcast_to([P, NT, nh])
                    u, m = tm[:, 0, :, 0:nh], tm[:, 1, :, 0:nh]
                    link(ve.tensor_tensor(arg[:, 2, :, 0:nh], d, top, ALU.subtract))
                    link(ve.tensor_tensor(u, s, top, ALU.add))
                    link(ve.tensor_scalar(arg[:, 3, :, 0:nh], arg[:, 2, :, 0:nh], SLOPE, None, ALU.mult))
                    link(ve.scalar_tensor_tensor(m, u, SLOPE, u, ALU.mult, ALU.max))
                    if which == 0:
                        link(ve.tensor_scalar(m, m, bcol[:, 3:4], None, ALU.add))
                        link(ve.scalar_tensor_tensor(arg[:, 0, :, 0:nh], u, bcol[:, 3:4], m, ALU.add,
                                                     ALU.subtract))
                        link(ve.tensor_scalar(u, u, SLOPE, bcol[:, 3:4], ALU.mult, ALU.add))
                        args_ready.by(ve.tensor_tensor(arg[:, 1, :, 0:nh], u, m, ALU.subtract))
                    else:
                        link(ve.tensor_tensor(arg[:, 0, :, 0:nh], u, m, ALU.subtract))
                        args_ready.by(ve.scalar_tensor_tensor(arg[:, 1, :, 0:nh], u, SLOPE, m, ALU.mult,
                                                              ALU.subtract))

                def split_high(nh, f, r, src, which):
                    ve.wait_ge(weights.sem, weights.at(b, which + 1))
                    va, _, _ = gat_views(nh, f)
                    wa = ew[:, 2, :, 0:nh].unsqueeze(3).broadcast_to([P, NT, nh, f])
                    link(ve.tensor_scalar(tm[:, 0, :, 0:nh], sd[:, :, nh:2 * nh], -1.0, None, ALU.mult))
                    link(ve.tensor_tensor(va, src, wa, ALU.mult))
                    link(ve.tensor_copy(r[:, :, :, 0, 0, :], va))
                    link(ve.tensor_tensor(va, va, r[:, :, :, 0, 0, :], ALU.subtract))
                    link(ve.tensor_copy(r[:, :, :, 0, 1, :], va))
                    ra_ready.by(ve.tensor_tensor(r[:, :, :, 0, 2, :], va, r[:, :, :, 0, 1, :], ALU.subtract))

                def steps(n, h, src):
                    for jt in range(NT):
                        k = n * NT + jt
                        if 8 <= k < NT * H1:
                            ve.wait_ge(step_used.sem, step_used.at(b, k - 7))
                        if jt < ACT_TILES:
                            m = n * ACT_TILES + jt
                            ve.wait_ge(sign_ready.sem, sign_ready.at(b, m + 1))
                            step_ready.by(ve.tensor_tensor(step[:, k % 8, :], sign[:, m % 4, :],
                                                           block_t[:, jt, :], ALU.is_gt))
                        else:
                            step_ready.by(ve.scalar_tensor_tensor(step[:, k % 8, :], src, tm[:, 0, jt, h:h + 1],
                                                                  mask_t[:, jt, :], ALU.is_gt, ALU.mult))

                def gat_sum(nh, f, g, dst, which):
                    tb, _, ts = gat_views(nh, f)
                    ta, tb = ts[:, :, :, 0, :], ts[:, :, :, 1, :]
                    wA = ew[:, 0, :, 0:nh].unsqueeze(3).broadcast_to([P, NT, nh, f])
                    wB = ew[:, 1, :, 0:nh].unsqueeze(3).broadcast_to([P, NT, nh, f])
                    link(ve.tensor_tensor(ta, ta, wA, ALU.mult))
                    if g is not None:
                        link(ve.tensor_tensor(tb, g, tb, ALU.subtract))
                    link(ve.tensor_tensor(tb, tb, wB, ALU.mult))
                    link(ve.tensor_tensor(ta, ta, tb, ALU.add))
                    e = empty[:, :].unsqueeze(2).broadcast_to([P, NT, nh * f]).rearrange(
                        "p t (h f) -> p t h f", h=nh)
                    c = csum[:, 0:nh * f].unsqueeze(1).broadcast_to([P, NT, nh * f]).rearrange(
                        "p t (h f) -> p t h f", h=nh)
                    ve.wait_ge(csum_out.sem, csum_out.at(b, which + 1))
                    link(ve.tensor_tensor(tb, e, c, ALU.mult))
                    link(ve.tensor_tensor(ta, ta, tb, ALU.add))
                    rd = rden[:, 0:NT * nh].rearrange("p (t h) -> p t h", h=nh)
                    link(ve.reciprocal(rd, ta[:, :, :, f - 1]))
                    return ve.tensor_tensor(dst, ta[:, :, :, 0:f - 1],
                                            rd.unsqueeze(3).broadcast_to([P, NT, nh, f - 1]), ALU.mult)

                ve.wait_ge(x_landed.sem, x_landed.at(b, 16))
                ln(xin, 0)
                low_parts(0)
                ve.wait_ge(v_ps.sem, v_ps.at(b, 1))
                bv = brow[:, BV:BV + 1, :].broadcast_to([P, NT, D]).rearrange("p t (h f) -> p t h f", h=H0)
                v_ready.by(ve.tensor_tensor(
                    v0[:, :, :, 0:DH0], ps[:, 4:6, :].rearrange("p a (t h f) -> p (a t) h f", h=H0, f=DH0), bv,
                    ALU.add))

                def share(m):
                    ve.wait_ge(pv0.sem, pv0.at(b, m + 1))
                    cols = slice((m % 2) * HALF, (m % 2 + 1) * HALF)
                    link(ve.reciprocal(inv0[:, cols], ps[:, 5 + 2 * (m % 2), :]))
                    if m >= 4:
                        ve.wait_ge(ctx0.sem, ctx0.at(b, m - 3))
                    dst = flat(bufc[:, :, :])[:, cols] if m < 2 else hT[:, cols]
                    share0.by(ve.tensor_tensor(dst, ps[:, 4 + 2 * (m % 2), :], inv0[:, cols], ALU.mult))

                for n in range(H0 * NT):
                    c, h = n // H0, n % H0
                    ve.wait_ge(s0_ready.sem, s0_ready.at(b, n + 1))
                    if c >= 2:
                        ve.wait_ge(pv0.sem, pv0.at(b, 2 * (c - 1)))
                    clip_ready.by(ve.scalar_tensor_tensor(
                        maps[:, n % 8, :], ps[:, 2 * (n % 2):2 * (n % 2) + 2, :].rearrange("p a n -> p (a n)"),
                        -CLIP, limit_t[:, c, :], ALU.max, ALU.min))
                    if c and h >= 2:
                        share(2 * (c - 1) + h - 2)
                share(2 * NT - 2)
                share(2 * NT - 1)
                ve.wait_ge(lin_ps.sem, lin_ps.at(b, 1))
                acc = ps[:, 4:6, :].rearrange("p a (t f) -> p (a t) f", f=D)
                link(ve.tensor_tensor(bufc[:, :, :], acc, hn[:, :, :], ALU.add))
                link(ve.tensor_tensor(bufc[:, :, :], bufc[:, :, :], row(BO), ALU.add))
                ln(bufc, 1)
                ve.wait_ge(normed.sem, normed.at(b, 1))
                link(ve.tensor_tensor(bufc[:, :, :], bufd[:, :, :], row(GAMMA), ALU.mult))
                link(ve.tensor_tensor(bufc[:, :, :], bufc[:, :, :], row(BETA), ALU.add))
                ve.wait_ge(x_stored.sem, x_stored.at(b, 0))
                x_freed.by(ve.tensor_tensor(xr[:, :, :], bufc[:, :, :], xin[:, :, :], ALU.add))
                ve.wait_ge(x_freed.sem, x_freed.at(b, 1))

                ln(xr, 2)
                ve.wait_ge(lin_ps.sem, lin_ps.at(b, 2))
                gat_out_of_psum(H1, F1, v1, D + 2 * H1)
                gat_weights(H1, 0)
                split_high(H1, F1, r1, v1[:, :, :, :], 0)
                ve.wait_ge(csum_ps.sem, csum_ps.at(b, 1))
                csum_out.by(ve.tensor_copy(csum[:, :], ps[:, 7, 0:H1 * F1]))

                def g_sums():
                    for it in range(NT):
                        ve.wait_ge(g_ps.sem, g_ps.at(b, it + 1))
                        acc = ps[:, 4 + it % 4, 0:H1 * 3 * F1].rearrange("p (h r f) -> p h f r", h=H1, r=3)
                        g_out.by(ve.tensor_reduce(gsum[:, it, :, :], acc, AX.X, ALU.add))

                def t_sums(h):
                    _, _, ts = gat_views(H1, F1)
                    ve.wait_ge(step_used.sem, step_used.at(b, NT * (h + 1)))
                    for half in range(2):
                        acc = ps[:, 4 + 2 * (h % 2) + half, 0:4 * 6 * F1].rearrange(
                            "p (t s r f) -> p t s f r", t=4, s=2, r=3)
                        ins = ve.tensor_reduce(ts[:, 4 * half:4 * half + 4, h, :, :], acc, AX.X, ALU.add)
                    t_out.by(ins)

                ve.wait_ge(rb_ready.sem, rb_ready.at(b, 1))
                for h in range(H1):
                    ve.wait_ge(rows_out.sem, rows_out.at(b, h + 1))
                    steps(h, h, sbc[:, h % 2, :])
                    if h == 0:
                        g_sums()
                    else:
                        t_sums(h - 1)
                t_sums(H1 - 1)
                ve.wait_ge(t_out.sem, t_out.at(b, H1))
                hn1_ready.by(gat_sum(H1, F1, gsum[:, :, :, :], bufc[:, :, :].rearrange(
                    "p t (h f) -> p t h f", h=H1), 0))
                ve.wait_ge(lin_ps.sem, lin_ps.at(b, 3))
                acc = ps[:, 4:6, :].rearrange("p a (t f) -> p (a t) f", f=D)
                link(ve.tensor_tensor(xr[:, :, :], acc, xr[:, :, :], ALU.add))

                ln(xr, 3)
                low_parts(1)
                ve.wait_ge(v_ps.sem, v_ps.at(b, 2))
                v_ready.by(ve.tensor_copy(v2[:, :, :, 0:DH1],
                                          ps[:, 4:6, :].rearrange("p a (t h f) -> p (a t) h f", h=H1, f=DH1)))
                for h in range(H1):
                    for a in range(2 * NT):
                        it, half = a // 2, a % 2
                        n = h * 2 * NT + a
                        ve.wait_ge(nat_ps.sem, nat_ps.at(b, n + 1))
                        if n >= 3:
                            ve.wait_ge(nat_used.sem, nat_used.at(b, n - 2))
                        carry(ve)
                        nat_used.by(ve.tensor_tensor_reduce(
                            junk[:, n % 3, :], ps[:, 6 + n % 2, :], block_n[:, it, half * HALF:(half + 1) * HALF],
                            1.0, -3.0e38, ALU.add, ALU.max, msplit[:, h % 2, it, half:half + 1]))
                    ve.wait_ge(nat_used.sem, nat_used.at(b, (h + 1) * 2 * NT))
                    if h >= 2:
                        ve.wait_ge(mrow_ps.sem, mrow_ps.at(b, h - 1))
                    link(ve.tensor_tensor(mtop[:, h % 2, :], msplit[:, h % 2, :, 0], msplit[:, h % 2, :, 1],
                                          ALU.max))
                    mneg_ready.by(ve.tensor_scalar(mneg[:, h % 2, :], mtop[:, h % 2, :], -1.0, None, ALU.mult))

                for q in range(H1 // 2):
                    ve.wait_ge(turned.sem, turned.at(b, 8 + 2 * q + 2))
                    for e in range(2):
                        h = 2 * q + e
                        acc = ps[:, 2 * (q % 2) + e, :].rearrange("p (k c s f) -> p s k f c", k=4, c=2, s=2)
                        for half in range(2):
                            ins = ve.tensor_reduce(
                                gsum[:, 4 * half:4 * half + 4, h, :], acc[:, half, :, 0:F1, :], AX.X, ALU.add)
                    ctx2_nat.by(ins)
                ve.wait_ge(ctx2_nat.sem, ctx2_nat.at(b, H1 // 2))
                rd = rden[:, :].rearrange("p (t h) -> p t h", h=H1)
                link(ve.reciprocal(rd, gsum[:, :, :, DH1]))
                link(ve.tensor_tensor(bufc[:, :, :].rearrange("p t (h f) -> p t h f", h=H1),
                                      gsum[:, :, :, 0:DH1], rd.unsqueeze(3).broadcast_to([P, NT, H1, DH1]),
                                      ALU.mult))
                link(ve.tensor_tensor(bufc[:, :, :], bufc[:, :, :], hn[:, :, :], ALU.add))
                ln(bufc, 4)
                ve.wait_ge(normed.sem, normed.at(b, 2))
                link(ve.tensor_tensor(bufc[:, :, :], bufd[:, :, :], row(G1), ALU.mult))
                x1_ready.by(ve.tensor_tensor(bufc[:, :, :], bufc[:, :, :], row(BE1), ALU.add))
                ve.wait_ge(lin_ps.sem, lin_ps.at(b, 5))
                acc = ps[:, 2:4, :].rearrange("p a (t f) -> p (a t) f", f=D)
                link(ve.tensor_tensor(bufc[:, :, :], acc, bufc[:, :, :], ALU.add))
                link(ve.tensor_tensor(bufc[:, :, :], bufc[:, :, :], row(B2), ALU.add))
                ln(bufc, 5)
                ve.wait_ge(normed.sem, normed.at(b, 3))
                link(ve.tensor_tensor(bufc[:, :, :], bufd[:, :, :], row(G2), ALU.mult))
                link(ve.tensor_tensor(bufc[:, :, :], bufc[:, :, :], row(BE2), ALU.add))
                link(ve.tensor_tensor(xr[:, :, :], xr[:, :, :], bufc[:, :, :], ALU.add))

                ln(xr, 6)
                ve.wait_ge(lin_ps.sem, lin_ps.at(b, 6))
                gat_out_of_psum(1, F3, v3, D + 2)
                gat_weights(1, 1)
                split_high(1, F3, r3, v3[:, :, :, :], 1)
                ve.wait_ge(csum_ps.sem, csum_ps.at(b, 2))
                csum_out.by(ve.tensor_copy(csum[:, 0:F3], ps[:, 3, 0:F3]))
                ve.wait_ge(rows_out.sem, rows_out.at(b, H1 + 1))
                steps(H1, 0, flat(bufd[:, :, :]))
                ve.wait_ge(step_ready.sem, step_ready.at(b, NT * (H1 + 1)))
                for jt in range(NT):
                    rest_ready.by(ve.tensor_tensor(rest[:, jt, :], mask_t[:, jt, :], step[:, jt, :],
                                                   ALU.subtract))
                ve.wait_ge(rb_ready.sem, rb_ready.at(b, 2))
                _, _, ts = gat_views(1, F3)
                for it in range(NT):
                    ve.wait_ge(t3_ps.sem, t3_ps.at(b, it + 1))
                    for s in range(2):
                        acc = ps[:, 4 + 2 * (it % 2) + s, 0:3 * F3].rearrange("p (r f) -> p f r", r=3)
                        ins = ve.tensor_reduce(ts[:, it, 0, s, :], acc, AX.X, ALU.add)
                    t3_out.by(ins)
                ve.wait_ge(t3_out.sem, t3_out.at(b, NT))
                link(gat_sum(1, F3, None, bufd[:, :, :].unsqueeze(2), 1))
                elu_ready.by(ve.tensor_scalar(bufc[:, :, :], bufd[:, :, :], 0.0, None, ALU.min))
                link(ve.tensor_scalar(bufd[:, :, :], bufd[:, :, :], 0.0, -1.0, ALU.max, ALU.add))
                link(ve.tensor_tensor(xr[:, :, :], xr[:, :, :], bufd[:, :, :], ALU.add))
                ve.wait_ge(act_free.sem, act_free.at(b, 1))
                x_done.by(ve.tensor_tensor(xr[:, :, :], xr[:, :, :], hn[:, :, :], ALU.add))
            assert chain[0] == dve.per, ("DVE_CHAIN", chain[0])

        @block.tensor
        def _(pe):
            pe.wait_ge(loaded.sem, 16 * len(LOADS))
            pe.wait_ge(set_pool.sem, 9)
            for n in range(5):
                ins = pe.transpose(ps[:, n // 4, (n % 4) * D:(n % 4 + 1) * D], raw_w[:, n, :], ident[:, :])
            ins.then_inc(set_pe.sem, 1)
            pe.wait_ge(set_dve.sem, setup_marks["nat"])
            for jt in range(NT):
                if jt >= 2:
                    pe.wait_ge(set_dve.sem, setup_marks["turn"] - NT + jt - 1)
                bank = ps[:, 2 + jt % 2, :].bitcast(BF16)
                for it in range(NT):
                    ins = pe.transpose(bank[:, it * P:(it + 1) * P], nat01[:, it, jt * P:(jt + 1) * P],
                                       ident_b[:, :])
                ins.then_inc(set_pe.sem, 1)
            pe.wait_ge(set_dve.sem, setup_marks["end"])

            with pe.Fori(0, B) as b:
                def turn(src, event):
                    for t in range(NT):
                        if callable(event):
                            event(t)
                        ins = pe.transpose(ps[:, 6 + t // 4, (t % 4) * P:(t % 4 + 1) * P], src(t), ident[:, :])
                        if t % 4 == 3:
                            turned.by(ins)

                def turn_h(m):
                    turn(lambda t: hn[:, t, :], lambda t: pe.wait_ge(h_tile.sem, h_tile.at(b, m * NT + t + 1)))

                def project(bank, lhsT, rhs=hT):
                    for half in range(2):
                        ins = pe.matmul(ps[:, bank + half, :], lhsT, rhs[:, half * HALF:(half + 1) * HALF],
                                        start=True, stop=True)
                    return ins

                def rows_of(src, rhs, bank, width, per_bank):
                    for t in range(NT):
                        at = (t % per_bank) * width
                        ins = pe.matmul(ps[:, bank + t // per_bank, at:at + width], src[:, t * P:(t + 1) * P],
                                        rhs, start=True, stop=True)
                    return ins

                def top_across(nh, which):
                    pe.wait_ge(top1.sem, top1.at(b, which + 1))
                    top1T.by(pe.transpose(ps[0:nh, 6, 0:P], dmx[:, 0:nh], ident[:, :]))
                    pe.wait_ge(top_diag.sem, top_diag.at(b, which + 1))
                    top_ps.by(pe.matmul(ps[:, 7, 0:nh], ones[0:nh, 0:P], dmdiag[0:nh, 0:nh], start=True, stop=True))

                turn_h(0)
                pe.wait_ge(actT.sem, actT.at(b, 2))
                qk_ps.by(project(0, wT[:, 0, :]))
                qk_ps.by(project(2, wT[:, 1, :]))
                v_ps.by(rows_of(hT, wT[:, 2, :], 4, D, 4))
                pe.wait_ge(parts_ready.sem, parts_ready.at(b, 2))
                pe.wait_ge(v_ready.sem, v_ready.at(b, 1))

                def scores0(n):
                    c, h = n // H0, n % H0
                    if c == 0:
                        pe.wait_ge(stack[h].sem, stack[h].at(b, 32 * sum(map(len, TERMS0))))
                    if n >= 2:
                        pe.wait_ge(clip_ready.sem, clip_ready.at(b, n - 1))
                    for half in range(2):
                        for s in range(2):
                            ins = pe.matmul(ps[:, 2 * (n % 2) + half, :],
                                            stk[0:K0[s], 2 * h + s, c * P:(c + 1) * P],
                                            stq[0:K0[s], 2 * h + s, half * HALF:(half + 1) * HALF],
                                            start=(s == 0), stop=(s == 1))
                    s0_ready.by(ins)

                def values0(m):
                    c, half = m // 2, m % 2
                    pe.wait_ge(p0_ready.sem, p0_ready.at(b, H0 * (c + 1)))
                    if m >= 2:
                        pe.wait_ge(share0.sem, share0.at(b, m - 1))
                    for what in range(2):
                        for h in range(H0):
                            ins = pe.matmul(ps[DH0 * h:DH0 * (h + 1), 4 + 2 * half + what, :],
                                            v0[:, c, h, :] if what == 0 else ones[:, 0:DH0],
                                            maps[:, (H0 * c + h) % 8, half * HALF:(half + 1) * HALF],
                                            start=True, stop=True)
                    pv0.by(ins)

                for n in range(H0):
                    scores0(n)
                for c in range(NT):
                    for half in range(2):
                        if c + 1 < NT:
                            scores0(H0 * (c + 1) + 2 * half)
                            scores0(H0 * (c + 1) + 2 * half + 1)
                        values0(2 * c + half)
                pe.wait_ge(ctx0.sem, ctx0.at(b, ctx0.per))
                lin_ps.by(rows_of(flat(bufc[:, :, :]), wT[:, 3, :], 4, D, 4))

                turn_h(1)
                pe.wait_ge(actT.sem, actT.at(b, 4))
                lin_ps.by(rows_of(hT, w1cat[:, :], 0, D + 2 * H1, 3))
                pe.wait_ge(lin_out.sem, lin_out.at(b, 1))

                def s_rows(n, cat, at, bank):
                    rows_ps.by(project(bank, cat[:, at:at + 1].broadcast_to([P, P])))

                s_rows(0, w1cat, D, 0)
                s_rows(1, w1cat, D + 1, 2)
                top_across(H1, 0)
                pe.wait_ge(args_ready.sem, args_ready.at(b, 1))
                for t in range(NT):
                    ins = pe.matmul(ps[:, 7, 0:H1 * F1], ones[:, 0:P], v1[:, t, :, :].rearrange("p h f -> p (h f)"),
                                    start=(t == 0), stop=(t == NT - 1))
                csum_ps.by(ins)
                pe.wait_ge(rb_ready.sem, rb_ready.at(b, 1))
                pe.wait_ge(ra_ready.sem, ra_ready.at(b, 1))
                pe.wait_ge(csum_out.sem, csum_out.at(b, 1))
                for it in range(NT):
                    if it >= 4:
                        pe.wait_ge(g_out.sem, g_out.at(b, it - 3))
                    for jt in range(NT):
                        ins = pe.matmul(ps[:, 4 + it % 4, 0:H1 * 3 * F1], mask_t[:, jt, it * P:(it + 1) * P],
                                        r1[:, jt, :, 1, :, :].rearrange("p h r f -> p h (r f)"),
                                        start=(jt == 0), stop=(jt == NT - 1))
                    g_ps.by(ins)
                for h in range(H1):
                    if h == 0:
                        pe.wait_ge(g_out.sem, g_out.at(b, NT))
                    if h >= 2:
                        pe.wait_ge(t_out.sem, t_out.at(b, h - 1))
                    for jt in range(NT):
                        k = h * NT + jt
                        pe.wait_ge(step_ready.sem, step_ready.at(b, k + 1))
                        for it in range(NT):
                            at = (it % 4) * 6 * F1
                            ins = pe.matmul(ps[:, 4 + 2 * (h % 2) + it // 4, at:at + 6 * F1],
                                            step[:, k % 8, it * P:(it + 1) * P],
                                            r1[:, jt, h, :, :, :].rearrange("p s r f -> p (s r f)"),
                                            start=(jt == 0 and it % 4 == 0), stop=(jt == NT - 1),
                                            skip_group_check=True)
                        step_used.by(ins)
                    if h + 2 < H1:
                        pe.wait_ge(rows_out.sem, rows_out.at(b, h + 1))
                        s_rows(h + 2, w1cat, D + h + 2, 2 * (h % 2))
                pe.wait_ge(hn1_ready.sem, hn1_ready.at(b, 1))
                turn(lambda t: bufc[:, t, :], None)
                pe.wait_ge(actT.sem, actT.at(b, 6))
                lin_ps.by(rows_of(flat(bufd[:, :, :]), wT[:, 4, :], 4, D, 4))

                turn_h(2)
                pe.wait_ge(actT.sem, actT.at(b, 8))
                qk_ps.by(project(0, wqkv[:, 0:D]))
                qk_ps.by(project(2, wqkv[:, D:2 * D]))
                v_ps.by(rows_of(hT, wqkv[:, 2 * D:3 * D], 4, D, 4))
                pe.wait_ge(parts_ready.sem, parts_ready.at(b, 4))
                pe.wait_ge(v_ready.sem, v_ready.at(b, 2))
                pe.wait_ge(ones_row.sem, ones_row.at(b, 16))

                def natural_scores(h, a):
                    n = h * 2 * NT + a
                    it, half = a // 2, a % 2
                    if a == 0:
                        pe.wait_ge(stack[h].sem, stack[h].at(
                            b, 32 * len(TERMS2) + (32 * sum(map(len, TERMS0)) if h < H0 else 0)))
                        if h:
                            pe.wait_ge(mrow_ready.sem, mrow_ready.at(b, h))
                    if n >= 2:
                        pe.wait_ge(nat_used.sem, nat_used.at(b, n - 1))
                    nat_ps.by(pe.matmul(ps[:, 6 + n % 2, :], stq[0:K2, h, it * P:(it + 1) * P],
                                        stk[0:K2, h, half * HALF:(half + 1) * HALF], start=True, stop=True))

                def max_row(h):
                    pe.wait_ge(mneg_ready.sem, mneg_ready.at(b, h + 1))
                    for it in range(NT):
                        ins = pe.matmul(ps[K2:K2 + 1, 6 + it // 4, (it % 4) * P:(it % 4 + 1) * P],
                                        mneg[:, h % 2, it:it + 1], ident_b[:, :], start=True, stop=True)
                    mrow_ps.by(ins)

                def scores2(n):
                    h, jt = n // NT, n % NT
                    if jt == 0:
                        pe.wait_ge(mrow_ready.sem, mrow_ready.at(b, h + 1))
                    if n >= 2:
                        pe.wait_ge(p2_ready.sem, p2_ready.at(b, n - 1))
                    for half in range(2):
                        cols = slice(half * HALF, (half + 1) * HALF)
                        pe.matmul(ps[:, 2 * (n % 2) + half, :], stk[0:K2 + 1, h, jt * P:(jt + 1) * P],
                                  stq[0:K2 + 1, h, cols], start=True, stop=False)
                        ins = pe.matmul(ps[:, 2 * (n % 2) + half, :], neg_ident_b[:, :], block_t[:, jt, cols],
                                        start=False, stop=True)
                    s2_ready.by(ins)

                def values2(m):
                    h, jt = m // 4, 2 * (m % 4)
                    pe.wait_ge(p2_ready.sem, p2_ready.at(b, 2 * m + 2))
                    if m % 4 == 0 and h >= 2:
                        pe.wait_ge(ctx2_out.sem, ctx2_out.at(b, h - 1))
                    for odd in range(2):
                        for half in range(2):
                            c = 32 * (2 * odd + half)
                            ins = pe.matmul(ps[c:c + 32, 4 + h % 2, :], v2[:, jt + odd, h, :],
                                            maps[:, (2 * m + odd) % 4, half * HALF:(half + 1) * HALF],
                                            start=(m % 4 == 0), stop=(m % 4 == 3))
                    pv2.by(ins)

                for a in range(2 * NT):
                    natural_scores(0, a)
                max_row(0)
                scores2(0)
                AHEAD = [3, 3, 3, 3, 2, 2, 0, 0]
                for h in range(H1):
                    a = 0
                    for jt in range(NT):
                        n = h * NT + jt
                        if h + 1 < H1:
                            for _ in range(AHEAD[jt]):
                                natural_scores(h + 1, a)
                                a += 1
                            if jt == NT - 2:
                                max_row(h + 1)
                        if n + 1 < H1 * NT:
                            scores2(n + 1)
                        if jt % 2:
                            values2(n // 2)
                for q in range(H1 // 2):
                    pe.wait_ge(ctx2_out.sem, ctx2_out.at(b, H1 if q == H1 // 2 - 1 else 2 * q + 2))
                    if q >= 2:
                        pe.wait_ge(ctx2_nat.sem, ctx2_nat.at(b, q - 1))
                    for e in range(2):
                        for k in range(4):
                            ins = pe.transpose(ps[:, 2 * (q % 2) + e, k * P:(k + 1) * P],
                                               ctx2[:, 2 * q + e, k * P:(k + 1) * P], ident[:, :])
                        turned.by(ins)
                pe.wait_ge(x1_ready.sem, x1_ready.at(b, 1))
                turn(lambda t: bufc[:, t, :], None)
                pe.wait_ge(actT.sem, actT.at(b, 10))
                lin_ps.by(project(0, ffn1[:, :]))
                pe.wait_ge(z_out.sem, z_out.at(b, 2))
                lin_ps.by(rows_of(flat(bufd[:, :, :]), ffn2[:, :], 2, D, 4))

                turn_h(3)
                pe.wait_ge(actT.sem, actT.at(b, 12))
                lin_ps.by(rows_of(hT, w3cat[:, :], 0, D + 2, 3))
                pe.wait_ge(lin_out.sem, lin_out.at(b, 2))
                s_rows(H1, w3cat, D, 0)
                top_across(1, 1)
                for t in range(NT):
                    ins = pe.matmul(ps[:, 3, 0:F3], ones[:, 0:P], v3[:, t, 0, :], start=(t == 0),
                                    stop=(t == NT - 1))
                csum_ps.by(ins)
                pe.wait_ge(rb_ready.sem, rb_ready.at(b, 2))
                pe.wait_ge(ra_ready.sem, ra_ready.at(b, 2))
                for it in range(NT):
                    if it >= 2:
                        pe.wait_ge(t3_out.sem, t3_out.at(b, it - 1))
                    for s in range(2):
                        for jt in range(NT):
                            if it == 0 and s == 0:
                                pe.wait_ge(step_ready.sem, step_ready.at(b, NT * H1 + jt + 1))
                            if it == 0 and s == 1:
                                pe.wait_ge(rest_ready.sem, rest_ready.at(b, jt + 1))
                            src = (step, rest)[s]
                            ins = pe.matmul(ps[:, 4 + 2 * (it % 2) + s, 0:3 * F3], src[:, jt, it * P:(it + 1) * P],
                                            r3[:, jt, 0, s, :, :].rearrange("p r f -> p (r f)"),
                                            start=(jt == 0), stop=(jt == NT - 1))
                    t3_ps.by(ins)

        for s in signals:
            if s.per and s.given != s.per:
                raise ValueError(f"{s.name}: {s.given} increments a batch, {s.per} stated")


DVE_CHAIN, POOL_CHAIN, ACT_CHAIN = 102, 8, 1
setup_marks = {}

_INS = ["x", "adj"] + ["L0_gnn_" + n for n in ("Wq", "bq", "Wk", "bk", "Wv", "bv", "Wo", "bo", "gamma", "beta")] + [
    "L1_gnn_" + n for n in ("W", "a_src", "a_dst", "beta_tilde", "W_out")] + [
    "L2_gnn_" + n for n in ("w_qkv", "ln1_g", "ln1_b", "ln2_g", "ln2_b", "w1", "b1", "w2", "b2")] + [
    "L3_gnn_" + n for n in ("W", "a")]


def kernel(**inputs):
    import numpy as np
    import concourse.bacc as bacc
    from concourse.bass_utils import run_bass_kernel_spmd

    nc = bacc.Bacc("TRN2", target_bir_lowering=False, num_devices=1)
    arrays, aps = {}, {}
    for name in _INS:
        a = np.ascontiguousarray(inputs[name])
        if a.ndim == 0:
            a = a.reshape(1)
        arrays[f"in_{name}"] = a
        aps[name] = nc.dram_tensor(f"in_{name}", a.shape, mybir.dt.from_np(a.dtype), kind="ExternalInput").ap()
    out = nc.dram_tensor("out_x", inputs["x"].shape, F32, kind="ExternalOutput").ap()
    program(nc, aps["x"], aps["adj"], aps, out, inputs["x"].shape[0])
    r = run_bass_kernel_spmd(nc, [arrays], core_ids=[0])
    return r.results[0]["out_x"]
```

```python
from contextlib import ExitStack

import concourse.bass as bass
from concourse import mybir

F32 = mybir.dt.float32
BF16 = mybir.dt.bfloat16
I32 = mybir.dt.int32
ALU = mybir.AluOpType
ACT = mybir.ActivationFunctionType
AX = mybir.AxisListType

P = 128
NT = 8
N = P * NT
D = 128
HALF = 512
H0, DH0 = 4, 32
H1, DH1 = 8, 16
BIG = float(2.0 ** 100)
EPS_LN = 1e-5
EPS_PRIOR = 1e-6
SLOPE = 0.2
CLIP = 10.0

TERMS0 = [[(0, 0), (0, 1), (1, 0), (0, 2)], [(2, 0), (1, 1), (1, 2)]]
TERMS2 = [(0, 0), (0, 1), (1, 0), (0, 2), (2, 0), (1, 1)]
K0 = [len(t) * DH0 for t in TERMS0]
K2 = len(TERMS2) * DH1
AHEAD = [3, 3, 3, 3, 2, 2, 0, 0]
POOL_SPLIT = 5
ACT_TILES = 6


class Signal:

    def __init__(self, nc, ctx, name, per_batch, before=0):
        self.name, self.per, self.given, self.before = name, per_batch, 0, before
        self.sem = ctx.enter_context(nc.semaphore(name))

    def at(self, b, count):
        return b * self.per + (count + self.before)

    def next(self, b, ahead, count):
        return self.at(b, count + ahead * self.per)

    def by(self, ins, n=1):
        self.given += n
        ins.then_inc(self.sem, n)
        return ins


def program(nc, x, adj, w, out, B):
    with ExitStack() as ctx:
        def sb(name, shape, dt=F32):
            return ctx.enter_context(nc.sbuf_tensor(name, shape, dt))

        def signal(name, per_batch, before=0):
            s = Signal(nc, ctx, name, per_batch, before)
            signals.append(s)
            return s

        signals = []
        ps = ctx.enter_context(nc.psum_tensor("ps", [P, 8, HALF], F32))

        ident = sb("ident", [P, P])
        ident_b = sb("ident_b", [P, P], BF16)
        neg_ident_b = sb("neg_ident_b", [P, P], BF16)
        ones = sb("ones", [P, H1 * (DH1 + 1)])
        ones_b = sb("ones_b", [1, N], BF16)
        tick = sb("tick", [1, 4])
        pick = sb("pick", [P, 2, DH0])
        neg_half = sb("neg_half", [P, NT])
        mask_t = sb("mask_t", [P, NT, N], BF16)
        limit_t = sb("limit_t", [P, NT, N], BF16)
        block_t = sb("block_t", [P, NT, N], BF16)
        block_n = sb("block_n", [P, NT, N], BF16)
        empty = sb("empty", [P, NT])
        wT = sb("wT", [P, 5, D])
        bcol = sb("bcol", [P, 4])
        brow = sb("brow", [P, 9, D])
        w1cat = sb("w1cat", [P, D + 2 * H1])
        w3cat = sb("w3cat", [P, D + 2])
        wqkv = sb("wqkv", [P, 3 * D])
        ffn1 = sb("ffn1", [P, D])
        ffn2 = sb("ffn2", [P, D])
        BV, BO, GAMMA, BETA, G1, BE1, G2, BE2, B2 = range(9)

        xin = sb("xin", [P, NT, D])
        xr = sb("xr", [P, NT, D])
        hn = sb("hn", [P, NT, D])
        hT = sb("hT", [P, N])
        bufc = sb("bufc", [P, NT, D])
        bufd = sb("bufd", [P, NT, D])
        parts = sb("parts", [P, 2, 3, N], BF16)
        arena = sb("arena", [P, 2, NT * HALF])
        maps = sb("maps", [P, NT, N])
        v2 = sb("v2", [P, NT, H1, 32])
        v1 = sb("v1", [P, NT, H1, DH1 + 1])
        v3 = sb("v3", [P, NT, 1, D + 1])
        gsum = sb("gsum", [P, NT, H1, DH1 + 1])
        csum = sb("csum", [P, H1 * (DH1 + 1)])
        stats = sb("stats", [P, NT, 6])
        mv = sb("mv", [P, NT, 2])
        rstd = sb("rstd", [P, NT])
        shift = sb("shift", [P, NT])
        early_stats = sb("early_stats", [P, NT, 6])
        early_mv = sb("early_mv", [P, NT, 2])
        early_rstd = sb("early_rstd", [P, NT])
        early_shift = sb("early_shift", [P, NT])
        sd = sb("sd", [P, NT, 2 * H1])
        dmx = sb("dmx", [P, H1])
        dmc = sb("dmc", [P, 1])
        dmdiag = sb("dmdiag", [P, H1])
        dmax = sb("dmax", [P, H1])
        arg = sb("arg", [P, 4, NT, H1])
        ew = sb("ew", [P, 4, NT, H1])
        tm = sb("tm", [P, 2, NT, H1])
        rden = sb("rden", [P, NT * H1])
        msplit = sb("msplit", [P, 2, NT, 2])
        mtop = sb("mtop", [P, 2, NT])
        mneg = sb("mneg", [P, 2, NT], BF16)
        junk = sb("junk", [P, 3, HALF], BF16)

        flat = lambda t: t.rearrange("p t f -> p (t f)")
        HT = NT // 2
        half_of = lambda t, g: t[:, g * HT:(g + 1) * HT, :]
        acc_half = lambda bank: ps[:, bank, :].rearrange("p (t f) -> p t f", f=D)
        WO_PS, IN1_PS, OUT1_PS, FFN1_PS, FFN2_PS, IN3_PS = 0, 2, 3, 5, 7, 9
        t3s = junk[:, :, :].rearrange("p a n -> p (a n)").bitcast(F32)[:, 0:4 * (D + 1)].rearrange(
            "p (a s f) -> p a s f", a=2, s=2)
        stq = arena[:, 0, :].bitcast(BF16).rearrange("p (h n) -> p h n", n=N)
        stk = arena[:, 1, :].bitcast(BF16).rearrange("p (h n) -> p h n", n=N)
        step = maps[:, 0:4, :].rearrange("p t n -> p (t n)").bitcast(BF16).rearrange("p (t n) -> p t n", n=N)
        rest = maps[:, 4:8, :].rearrange("p t n -> p (t n)").bitcast(BF16).rearrange("p (t n) -> p t n", n=N)
        sbc = maps[:, 4:6, :]
        resid = maps[:, 0:2, :]
        resid0 = (hT[:, :], flat(bufc[:, :, :]))
        ctx2 = maps[:, 4:8, :].rearrange("p t (s n) -> p (t s) n", n=HALF)
        sign = parts[:, :, :, :].rearrange("p a b n -> p (a b) n")[:, 0:4, :]
        F1 = DH1 + 1
        F3 = D + 1
        kview = arena[:, 1, :].bitcast(BF16)
        r1 = kview[:, 0:NT * H1 * 6 * F1].rearrange("p (t h s r f) -> p t h s r f", h=H1, s=2, r=3, f=F1)
        r3 = kview[:, 0:NT * 6 * F3].rearrange("p (t h s r f) -> p t h s r f", h=1, s=2, r=3, f=F3)

        def qview(at, nh, f):
            return arena[:, 0, at:at + NT * nh * f].rearrange("p (t h f) -> p t h f", h=nh, f=f)

        def gat_views(nh, f):
            n = NT * nh * f
            return (qview(0, nh, f), qview(n, nh, f),
                    arena[:, 0, 0:2 * n].rearrange("p (t h s f) -> p t h s f", h=nh, s=2, f=f))

        lone = v1[:, :, :, :].rearrange("p t h f -> p t (h f)")
        v0 = v1[:, :, :, :].rearrange("p t h f -> p (t h f)")[:, 0:NT * D].rearrange(
            "p (t h f) -> p t h f", h=H0, f=DH0)
        inv0 = (flat(bufd[:, :, :]), hT[:, :])
        num0 = gsum[:, :, :, :].rearrange("p t h f -> p (t h f)")[:, 0:N]
        den_t = junk[:, :, :].rearrange("p a n -> p (a n)").bitcast(F32)[:, 0:HALF]

        x_landed = signal("x_landed", 16)
        x_freed = signal("x_freed", 2)
        x_done = signal("x_done", 2)
        x_stored = signal("x_stored", 16, before=1)
        ln_var = signal("ln_var", 1 + 2 * 6)
        ln_rstd = signal("ln_rstd", 1 + 2 * 6)
        ln_coef = signal("ln_coef", 1 + 2 * 3)
        h_tile = signal("h_tile", 4 * NT)
        turned = signal("turned", 2 * 6 + 2 * H1 // 2)
        actT = signal("actT", 2 * 6)
        qk_ps = signal("qk_ps", 4)
        v_ps = signal("v_ps", 2)
        part_h = signal("part_h", 4)
        parts_ready = signal("parts_ready", 4)
        v_ready = signal("v_ready", 2)
        stack = [signal(f"stack{h}", 16 * (2 * len(TERMS0[0]) * (h < H0) + 2 * len(TERMS2)))
                 for h in range(H1)]
        s0_ready = signal("s0_ready", H0 * NT)
        clip_ready = signal("clip_ready", H0 * NT)
        p0_ready = signal("p0_ready", H0 * NT)
        den0 = signal("den0", NT)
        inv_ready = signal("inv_ready", NT)
        pv0 = signal("pv0", NT)
        sums0 = signal("sums0", NT - 1)
        share0 = signal("share0", NT - 1)
        ctx0 = signal("ctx0", NT - 2)
        ctx0_done = signal("ctx0_done", 2)
        lin_ps = signal("lin_ps", 10)
        lin_out = signal("lin_out", 2)
        top1 = signal("top1", 2)
        top1T = signal("top1T", 2)
        top_diag = signal("top_diag", 2)
        top_ps = signal("top_ps", 2)
        args_ready = signal("args_ready", 2)
        weights = signal("weights", 2)
        rows_ps = signal("rows_ps", H1 + 1)
        rows_out = signal("rows_out", H1 + 1)
        sign_ready = signal("sign_ready", ACT_TILES * (H1 + 1))
        step_ready = signal("step_ready", NT * (H1 + 1))
        step_used = signal("step_used", NT * H1)
        rest_ready = signal("rest_ready", NT)
        ra_ready = signal("ra_ready", 2)
        rb_ready = signal("rb_ready", 3)
        csum_ps = signal("csum_ps", 2)
        csum_out = signal("csum_out", 2)
        g_ps = signal("g_ps", NT)
        g_out = signal("g_out", NT)
        t_out = signal("t_out", H1)
        t3_ps = signal("t3_ps", NT)
        t3_out = signal("t3_out", NT)
        hn1_ready = signal("hn1_ready", 2)
        nat_ps = signal("nat_ps", H1 * NT * 2)
        nat_used = signal("nat_used", H1 * NT * 2)
        mneg_ready = signal("mneg_ready", H1)
        mrow_ps = signal("mrow_ps", H1)
        mrow_ready = signal("mrow_ready", H1)
        ones_row = signal("ones_row", 16)
        s2_ready = signal("s2_ready", H1 * NT)
        p2_ready = signal("p2_ready", H1 * NT)
        pv2 = signal("pv2", H1 * NT // 2)
        ctx2_out = signal("ctx2_out", H1)
        ctx2_nat = signal("ctx2_nat", H1 // 2)
        x1_ready = signal("x1_ready", 2)
        plus_row = signal("plus_row", 4)
        mixed = signal("mixed", H1)
        elu_ready = signal("elu_ready", 2)
        elu_exp = signal("elu_exp", 2)
        z_out = signal("z_out", 2)
        dve = signal("dve_chain", DVE_CHAIN)
        dve_early = signal("dve_early_chain", 6)
        pool = signal("pool_chain", POOL_CHAIN)
        loaded = signal("loaded", 0)
        set_pool = signal("set_pool", 0)
        set_dve = signal("set_dve", 0)
        set_pe = signal("set_pe", 0)
        set_act = signal("set_act", 0)

        block = ctx.enter_context(nc.Block())

        carried = [0]

        def carry(ve):
            carried[0] += 1
            ve.memset(tick[0:1, carried[0] % 4:carried[0] % 4 + 1], 0.0)

        x_v = x.rearrange("b (t p) f -> b p t f", p=P)
        out_v = out.rearrange("b (t p) f -> b p t f", p=P)
        adj_i = maps[:, :, :].bitcast(I32)
        nat01 = arena[:, :, :].rearrange("p a n -> p (a n)").bitcast(BF16)[:, 0:NT * N].rearrange(
            "p (t n) -> p t n", n=N)
        raw_w = bufc[:, 0:5, :]
        a_row = bufd[:, 0:4, :]
        a_tmp = hn[:, :, :]
        beta_c = shift[:, 0:1]

        LOADS = [
            (adj_i[:, :, :], adj.rearrange("(t p) n -> p t n", p=P)),
            (raw_w[:, 0, :], w["L0_gnn_Wq"]), (raw_w[:, 1, :], w["L0_gnn_Wk"]),
            (raw_w[:, 2, :], w["L0_gnn_Wv"]), (raw_w[:, 3, :], w["L0_gnn_Wo"]),
            (raw_w[:, 4, :], w["L1_gnn_W_out"]),
            (w1cat[:, 0:D].rearrange("p (h f) -> p h f", f=DH1), w["L1_gnn_W"].rearrange("h d f -> d h f")),
            (w3cat[:, 0:D], w["L3_gnn_W"]), (wqkv[:, :], w["L2_gnn_w_qkv"]),
            (ffn1[:, :], w["L2_gnn_w1"]), (ffn2[:, :], w["L2_gnn_w2"]),
            (bcol[:, 0:1], w["L0_gnn_bq"].rearrange("(p a) -> p a", a=1)),
            (bcol[:, 1:2], w["L0_gnn_bk"].rearrange("(p a) -> p a", a=1)),
            (bcol[:, 2:3], w["L2_gnn_b1"].rearrange("(p a) -> p a", a=1)),
            (a_row[:, 0, :], w["L1_gnn_a_src"].rearrange("h f -> (h f)").partition_broadcast(P)),
            (a_row[:, 1, :], w["L1_gnn_a_dst"].rearrange("h f -> (h f)").partition_broadcast(P)),
            (a_row[:, 2:4, :].rearrange("p a f -> p (a f)"),
             w["L3_gnn_a"].rearrange("n a -> (n a)").partition_broadcast(P)),
            (beta_c, w["L1_gnn_beta_tilde"].partition_broadcast(P)),
        ] + [(brow[:, n, :], w[name].partition_broadcast(P)) for n, name in enumerate(
            ["L0_gnn_bv", "L0_gnn_bo", "L0_gnn_gamma", "L0_gnn_beta", "L2_gnn_ln1_g", "L2_gnn_ln1_b",
             "L2_gnn_ln2_g", "L2_gnn_ln2_b", "L2_gnn_b2"])]

        def copy_stack(sp, h, term, rows, side, part, base, slot):
            st = (stq, stk)[side]
            stack[h].by(sp.dma_start(st[term * rows:(term + 1) * rows, slot, :],
                                     parts[base:base + rows, side, part, :]), 16)

        @block.sync
        def _(sp):
            for dst, src in LOADS:
                loaded.by(sp.dma_start(dst, src), 16)
            sp.wait_ge(set_pool.sem, 13)
            x_landed.by(sp.dma_start(xin[:, :, :], x_v[0]), 16)

            def stacks0(b, ahead, side):
                sp.wait_ge(parts_ready.sem, parts_ready.next(b, ahead, side + 1))
                if ahead:
                    if side == 0:
                        sp.wait_ge(ra_ready.sem, ra_ready.at(b, 2))
                        sp.wait_ge(rb_ready.sem, rb_ready.at(b, 3))
                    else:
                        sp.wait_ge(t3_ps.sem, t3_ps.at(b, NT))
                for h in range(H0):
                    for t, pair in enumerate(TERMS0[0]):
                        src = parts[h * DH0:(h + 1) * DH0, side, :, :]
                        first = pair[side]
                        if t < len(TERMS0[1]):
                            gap = TERMS0[1][t][side] - first
                            src = (src[:, first:first + gap + 1:gap, :] if gap
                                   else src[:, first:first + 1, :].broadcast_to([DH0, 2, N]))
                            dst = (stq, stk)[side][t * DH0:(t + 1) * DH0, 2 * h:2 * h + 2, :]
                        else:
                            src = src[:, first, :]
                            dst = (stq, stk)[side][t * DH0:(t + 1) * DH0, 2 * h, :]
                        stack[h].by(sp.dma_start(dst, src), 16)

            def batch(b, last):
                if not last:
                    sp.wait_ge(x_freed.sem, x_freed.at(b, 2))
                    x_landed.by(sp.dma_start(xin[:, :, :], x_v[b + 1]), 16)
                sp.wait_ge(part_h.sem, part_h.at(b, 4))
                for h, high in [(0, True), (0, False)] + [(h, None) for h in range(1, H1)]:
                    if (h, high) == (0, False):
                        sp.wait_ge(parts_ready.sem, parts_ready.at(b, 4))
                    for t, pair in enumerate(TERMS2):
                        for side in range(2):
                            if high is None or high == (pair[side] == 0):
                                copy_stack(sp, h, t, DH1, side, pair[side], h * DH1, h)
                    if (h, high) == (0, False):
                        ones_row.by(sp.dma_start(stk[K2:K2 + 1, :, :],
                                                 ones_b[0:1, :].unsqueeze(1).broadcast_to([1, H1, N])), 16)
                if not last:
                    stacks0(b, 1, 0)
                    stacks0(b, 1, 1)
                sp.wait_ge(x_done.sem, x_done.at(b, 2))
                x_stored.by(sp.dma_start(out_v[b], xr[:, :, :]), 16)

            stacks0(0, 0, 0)
            stacks0(0, 0, 1)
            if B > 1:
                with sp.Fori(0, B - 1) as b:
                    batch(b, False)
            batch(B - 1, True)
            sp.wait_ge(x_stored.sem, x_stored.at(B, 0))

        @block.gpsimd
        def _(gp):
            set_pool.by(gp.memset(ident[:, :], 0.0))
            set_pool.by(gp.memset(ones[:, :], 1.0))
            set_pool.by(gp.memset(ones_b[:, :], 1.0))
            set_pool.by(gp.memset(neg_half[:, :], -0.5))
            for n in range(4):
                set_pool.by(gp.memset(pick[:, n // 2, (n % 2) * (DH0 // 2):(n % 2 + 1) * (DH0 // 2)],
                                      float(n in (0, 3))))
            set_pool.by(gp.memset(v1[:, :, :, DH1:F1], 1.0))
            set_pool.by(gp.memset(v3[:, :, :, D:F3], 1.0))
            set_pool.by(gp.memset(v2[:, :, :, DH1:F1], 1.0))
            set_pool.by(gp.memset(v2[:, :, :, F1:32], 0.0))
            gp.wait_ge(set_pool.sem, 12)
            set_pool.by(gp.affine_select(out=ident[:, :], in_=ident[:, :], compare_op=ALU.not_equal, fill=1.0,
                                         base=0, pattern=[[-1, P]], channel_multiplier=1))
            chain = [0]

            def early_root(b, ahead):
                gp.wait_ge(ln_var.sem, ln_var.next(b, ahead, 1))
                ln_rstd.by(gp.tensor_tensor(early_rstd[:, :], early_mv[:, :, 1], neg_half[:, :], ALU.pow))

            def batch(b, last):
                chain[0] = 0

                def link(ins):
                    chain[0] += 1
                    pool.by(ins)
                    gp.wait_ge(pool.sem, pool.at(b, chain[0]))

                def inv_root(k):
                    for g in range(2):
                        gp.wait_ge(ln_var.sem, ln_var.at(b, 2 * k + g))
                        tiles = slice(g * HT, (g + 1) * HT)
                        ln_rstd.by(gp.tensor_tensor(rstd[:, tiles], mv[:, tiles, 1], neg_half[:, tiles], ALU.pow))

                def split_low(nh, f, r, src, which, n):
                    gp.wait_ge(weights.sem, weights.at(b, which + 1))
                    vb, r, src = gat_views(nh, f)[1][:, 0:n], r[:, 0:n], src[:, 0:n]
                    wb = ew[:, 3, 0:n, 0:nh].unsqueeze(3).broadcast_to([P, n, nh, f])
                    link(gp.tensor_tensor(vb, src, wb, ALU.mult))
                    one = ones[:, 0:nh * f].rearrange("p (h f) -> p h f", h=nh).unsqueeze(1).broadcast_to(
                        [P, n, nh, f])
                    link(gp.tensor_tensor(r[:, :, :, 1, 0, :], vb, one, ALU.mult))
                    link(gp.tensor_tensor(vb, vb, r[:, :, :, 1, 0, :], ALU.subtract))
                    link(gp.tensor_tensor(r[:, :, :, 1, 1, :], vb, one, ALU.mult))
                    rb_ready.by(gp.tensor_tensor(r[:, :, :, 1, 2, :], vb, r[:, :, :, 1, 1, :], ALU.subtract))

                def add_row(dst, src, v):
                    plus_row.by(gp.tensor_tensor(dst[:, :, :], src[:, :, :],
                                                 brow[:, v:v + 1, :].broadcast_to([P, NT, D]), ALU.add))

                gp.wait_ge(h_tile.sem, h_tile.at(b, NT))
                gp.wait_ge(turned.sem, turned.at(b, 2))
                add_row(hn, hn, BO)
                add_row(xin, xin, BETA)
                for c in range(NT - 1):
                    total = flat(bufc[:, :, :])
                    gp.wait_ge(inv_ready.sem, inv_ready.at(b, c + 1))
                    gp.wait_ge(sums0.sem, sums0.at(b, c + 1))
                    share0.by(gp.tensor_tensor(inv0[c % 2] if c else total, num0, inv0[c % 2], ALU.mult))
                    gp.wait_ge(share0.sem, share0.at(b, c + 1))
                    if c:
                        if c >= 2:
                            gp.wait_ge(ctx0.sem, ctx0.at(b, c - 1))
                        ctx0.by(gp.tensor_tensor(total, total, inv0[c % 2], ALU.add))
                inv_root(1)
                inv_root(2)
                split_low(H1, F1, r1, v1[:, :, :, :], 0, POOL_SPLIT)
                gp.wait_ge(csum_out.sem, csum_out.at(b, 1))
                gp.wait_ge(ra_ready.sem, ra_ready.at(b, 1))
                gp.wait_ge(rb_ready.sem, rb_ready.at(b, 2))
                link(gp.tensor_tensor(
                    lone[:, :, :], empty[:, :].unsqueeze(2).broadcast_to([P, NT, H1 * F1]),
                    csum[:, :].unsqueeze(1).broadcast_to([P, NT, H1 * F1]), ALU.mult))
                gp.wait_ge(g_out.sem, g_out.at(b, NT))
                for h in range(H1):
                    gp.wait_ge(t_out.sem, t_out.at(b, h + 1))
                    ts = gat_views(H1, F1)[2]
                    ta, tb = ts[:, :, h, 0, :], ts[:, :, h, 1, :]
                    wA, wB = (ew[:, k, :, h:h + 1].broadcast_to([P, NT, F1]) for k in range(2))
                    link(gp.tensor_tensor(tb, gsum[:, :, h, :], tb, ALU.subtract))
                    link(gp.tensor_tensor(ta, ta, wA, ALU.mult))
                    link(gp.tensor_tensor(tb, tb, wB, ALU.mult))
                    link(gp.tensor_tensor(ta, ta, lone[:, :, h * F1:(h + 1) * F1], ALU.add))
                    mixed.by(gp.tensor_tensor(ta, ta, tb, ALU.add))
                inv_root(3)
                gp.wait_ge(h_tile.sem, h_tile.at(b, 3 * NT))
                add_row(xr, xr, BE2)
                inv_root(4)
                gp.wait_ge(x1_ready.sem, x1_ready.at(b, 2))
                add_row(hn, bufc, B2)
                inv_root(5)
                inv_root(6)
                if not last:
                    early_root(b, 1)
                split_low(1, F3, r3, v3[:, :, :, :], 1, NT)
                assert chain[0] == pool.per, ("POOL_CHAIN", chain[0])

            early_root(0, 0)
            if B > 1:
                with gp.Fori(0, B - 1) as b:
                    batch(b, False)
            batch(B - 1, True)

        @block.scalar
        def _(act):
            act.wait_ge(loaded.sem, 16 * len(LOADS))
            set_act.by(act.activation(tm[:, 0, 0, 0:1], beta_c, ACT.Abs))
            act.wait_ge(set_act.sem, 1)
            set_act.by(act.activation(tm[:, 0, 1, 0:1], tm[:, 0, 0, 0:1], ACT.Exp, scale=-1.0))
            act.wait_ge(set_act.sem, 2)
            act.wait_ge(set_dve.sem, 1)
            act.wait_ge(set_pool.sem, 13)
            set_act.by(act.activation(tm[:, 0, 2, 0:1], tm[:, 0, 1, 0:1], ACT.Ln, bias=ones[:, 0:1]))
            set_act.by(act.activation(tm[:, 0, 3, 0:1], tm[:, 0, 4, 0:1], ACT.Ln))

            def early_norm(b, ahead):
                act.wait_ge(ln_coef.sem, ln_coef.next(b, ahead, 1))
                for t in range(NT):
                    h_tile.by(act.activation(hn[:, t, :], xin[:, t, :], ACT.Relu, bias=early_shift[:, t:t + 1],
                                             scale=early_rstd[:, t:t + 1]))

            def early_turn_out(b, ahead):
                for half in range(2):
                    act.wait_ge(turned.sem, turned.next(b, ahead, half + 1))
                    actT.by(act.copy(hT[:, half * HALF:(half + 1) * HALF], ps[:, 6 + half, :]))

            def early_high_parts(b, ahead):
                for u in range(2):
                    act.wait_ge(qk_ps.sem, qk_ps.next(b, ahead, u + 1))
                    if ahead and u == 0:
                        act.wait_ge(step_ready.sem, step_ready.at(b, NT * (H1 + 1)))
                    part_h.by(act.activation(parts[:, u, 0, :].rearrange("p (a n) -> p a n", a=2),
                                             ps[:, 2 * u:2 * u + 2, :], ACT.Identity, bias=bcol[:, u:u + 1]))

            def batch(b, last):
                def norm_relu(c):
                    for g in range(2):
                        act.wait_ge(ln_coef.sem, ln_coef.at(b, 2 * (c + 1) + g))
                        for t in range(g * HT, (g + 1) * HT):
                            h_tile.by(act.activation(hn[:, t, :], xr[:, t, :], ACT.Relu, bias=shift[:, t:t + 1],
                                                     scale=rstd[:, t:t + 1]))

                def turn_out(dst, event, m):
                    for half in range(2):
                        act.wait_ge(turned.sem, turned.at(b, event + half + 1))
                        actT.by(act.copy(dst[:, half * HALF:(half + 1) * HALF], ps[:, 6 + half, :]))

                def high_parts():
                    for u in range(2):
                        act.wait_ge(qk_ps.sem, qk_ps.at(b, 2 + u + 1))
                        part_h.by(act.copy(parts[:, u, 0, :].rearrange("p (a n) -> p a n", a=2),
                                           ps[:, 2 * u:2 * u + 2, :]))

                def rows(n, bank, dst):
                    act.wait_ge(rows_ps.sem, rows_ps.at(b, n + 1))
                    if 2 <= n < H1:
                        act.wait_ge(step_ready.sem, step_ready.at(b, NT * (n - 1)))
                    rows_out.by(act.copy(dst.rearrange("p (a n) -> p a n", a=2), ps[:, bank:bank + 2, :]))

                def signs(n, jts, src, nh, h):
                    act.wait_ge(rows_out.sem, rows_out.at(b, n + 1))
                    for jt in jts:
                        k = n * ACT_TILES + jt
                        if k >= 4:
                            old = k - 4
                            act.wait_ge(step_ready.sem, step_ready.at(
                                b, old // ACT_TILES * NT + old % ACT_TILES + 1))
                        sign_ready.by(act.activation(sign[:, k % 4, :], src, ACT.Sign,
                                                     bias=sd[:, jt, nh + h:nh + h + 1]))

                def sums_out(c):
                    act.wait_ge(pv0.sem, pv0.at(b, c + 1))
                    if c:
                        act.wait_ge(share0.sem, share0.at(b, c))
                    sums0.by(act.copy(num0.rearrange("p (a n) -> p a n", a=2), ps[:, 4:6, :]))

                for n in range(H0 * NT):
                    act.wait_ge(clip_ready.sem, clip_ready.at(b, n + 1))
                    p0_ready.by(act.activation(maps[:, n % 8, :], maps[:, n % 8, :], ACT.Exp))
                    if n >= H0 and n % H0 == H0 - 1:
                        sums_out(n // H0 - 1)
                norm_relu(0)
                turn_out(hT, 2, 1)
                act.wait_ge(lin_out.sem, lin_out.at(b, 1))
                rows(0, 0, sbc[:, 0, :])
                signs(0, range(4), sbc[:, 0, :], H1, 0)
                act.wait_ge(args_ready.sem, args_ready.at(b, 1))
                weights.by(act.activation(ew[:, :, :, :], arg[:, :, :, :], ACT.Exp))
                signs(0, range(4, ACT_TILES), sbc[:, 0, :], H1, 0)
                for h in range(1, H1):
                    rows(h, 2 * (h % 2), sbc[:, h % 2, :])
                    signs(h, range(ACT_TILES), sbc[:, h % 2, :], H1, h)
                turn_out(flat(bufd[:, :, :]), 4, 2)
                norm_relu(1)
                turn_out(hT, 6, 3)
                high_parts()
                for h in range(H1):
                    def max_row(h):
                        act.wait_ge(mrow_ps.sem, mrow_ps.at(b, h + 1))
                        mrow_ready.by(act.copy(stq[K2:K2 + 1, h, :].rearrange("p (a n) -> p a n", a=2),
                                               ps[K2:K2 + 1, 6:8, :]))

                    if h == 0:
                        max_row(0)
                    for jt in range(NT):
                        n = h * NT + jt
                        act.wait_ge(s2_ready.sem, s2_ready.at(b, n + 1))
                        if n >= 4:
                            act.wait_ge(pv2.sem, pv2.at(b, (n - 4) // 2 + 1))
                        p2_ready.by(act.activation(maps[:, n % 4, :].rearrange("p (a n) -> p a n", a=2),
                                                   ps[:, 2 * (n % 2):2 * (n % 2) + 2, :], ACT.Exp))
                        if jt == 1 and h > 0:
                            act.wait_ge(pv2.sem, pv2.at(b, NT // 2 * h))
                            ctx2_out.by(act.copy(ctx2[:, h - 1, :], ps[:, 4 + (h - 1) % 2, :]))
                        if jt == NT - 2 and h + 1 < H1:
                            max_row(h + 1)
                act.wait_ge(pv2.sem, pv2.at(b, NT // 2 * H1))
                ctx2_out.by(act.copy(ctx2[:, H1 - 1, :], ps[:, 4 + (H1 - 1) % 2, :]))
                turn_out(hT, 8 + H1, 4)
                for half in range(2):
                    act.wait_ge(lin_ps.sem, lin_ps.at(b, FFN1_PS + half + 1))
                    z_out.by(act.activation(flat(bufd[:, 4 * half:4 * half + 4, :]), ps[:, half, :], ACT.Relu,
                                            bias=bcol[:, 2:3]))
                norm_relu(2)
                turn_out(hT, 10 + H1, 5)
                if not last:
                    early_norm(b, 1)
                act.wait_ge(lin_out.sem, lin_out.at(b, 2))
                rows(H1, 0, flat(bufd[:, :, :]))
                signs(H1, range(4), flat(bufd[:, :, :]), 1, 0)
                act.wait_ge(args_ready.sem, args_ready.at(b, 2))
                weights.by(act.activation(ew[:, :, :, 0:1], arg[:, :, :, 0:1], ACT.Exp))
                if not last:
                    early_turn_out(b, 1)
                signs(H1, range(4, ACT_TILES), flat(bufd[:, :, :]), 1, 0)
                if not last:
                    early_high_parts(b, 1)
                for g in range(2):
                    act.wait_ge(elu_ready.sem, elu_ready.at(b, g + 1))
                    elu_exp.by(act.activation(half_of(bufc, g), half_of(bufc, g), ACT.Exp))

            early_norm(0, 0)
            early_turn_out(0, 0)
            early_high_parts(0, 0)
            if B > 1:
                with act.Fori(0, B - 1) as b:
                    batch(b, False)
            batch(B - 1, True)

        @block.vector
        def _(ve):
            chain = [0]

            ve.wait_ge(loaded.sem, 16 * len(LOADS))
            ve.memset(tm[:, 0, 4, 0:1], 1.0 + EPS_PRIOR).then_inc(set_dve.sem, 1)
            ve.wait_ge(set_pool.sem, 13)
            done = [1]

            def seq(ins):
                done[0] += 1
                ins.then_inc(set_dve.sem, 1)
                ve.wait_ge(set_dve.sem, done[0])

            seq(ve.tensor_copy(ident_b[:, :], ident[:, :]))
            seq(ve.tensor_scalar(neg_ident_b[:, :], ident[:, :], -1.0, None, ALU.mult))
            seq(ve.tensor_scalar(nat01[:, :, :], adj_i[:, :, :], 0.0, None, ALU.is_gt))
            seq(ve.tensor_reduce(rden[:, 0:NT], nat01[:, :, :], AX.X, ALU.add))
            seq(ve.tensor_scalar(empty[:, :], rden[:, 0:NT], 0.0, None, ALU.is_equal))
            seq(ve.tensor_scalar(block_n[:, :, :], nat01[:, :, :], -1.0, BIG, ALU.add, ALU.mult))
            NAT_SET = done[0]
            for n, (wc, nh, f) in enumerate(((w1cat, H1, DH1), (w1cat, H1, DH1), (w3cat, 1, D), (w3cat, 1, D))):
                seq(ve.tensor_tensor(a_tmp[:, n, :], wc[:, 0:D], a_row[:, n, :], ALU.mult))
                at = D + (n % 2) * nh
                seq(ve.tensor_reduce(wc[:, at:at + nh], a_tmp[:, n, :].rearrange("p (h f) -> p h f", f=f),
                                     AX.X, ALU.add))
            seq(ve.tensor_scalar(wqkv[:, 0:D], wqkv[:, 0:D], DH1 ** -0.5, None, ALU.mult))
            seq(ve.tensor_scalar(bcol[:, 0:1], bcol[:, 0:1], DH0 ** -0.5, None, ALU.mult))
            ve.wait_ge(set_act.sem, 4)
            seq(ve.tensor_scalar(tm[:, 0, 5, 0:1], beta_c, 0.0, None, ALU.max))
            seq(ve.tensor_tensor(tm[:, 0, 6, 0:1], tm[:, 0, 5, 0:1], tm[:, 0, 2, 0:1], ALU.add))
            seq(ve.tensor_tensor(bcol[:, 3:4], tm[:, 0, 6, 0:1], tm[:, 0, 3, 0:1], ALU.mult))
            ve.wait_ge(set_pe.sem, 1)
            seq(ve.tensor_scalar(wT[:, 0, :], ps[:, 0, 0:D], DH0 ** -0.5, None, ALU.mult))
            seq(ve.tensor_copy(wT[:, 1:4, :], ps[:, 0, D:4 * D].rearrange("p (a f) -> p a f", a=3)))
            seq(ve.tensor_copy(wT[:, 4, :], ps[:, 1, 0:D]))
            for jt in range(NT):
                ve.wait_ge(set_pe.sem, 2 + jt)
                seq(ve.tensor_copy(mask_t[:, jt, :], ps[:, 2 + jt % 2, :].bitcast(BF16)))
            TURN_SET = done[0]
            seq(ve.tensor_scalar(limit_t[:, :, :], mask_t[:, :, :], 2 * CLIP, -CLIP, ALU.mult, ALU.add))
            seq(ve.tensor_scalar(block_t[:, :, :], mask_t[:, :, :], -BIG, BIG, ALU.mult, ALU.add))
            setup_marks.update(nat=NAT_SET, turn=TURN_SET, end=done[0])

            ve.memset(tick[0:1, 2:3], 0.0).then_inc(x_stored.sem, 1)

            def early_link(b, ahead, n, ins):
                dve_early.by(ins)
                ve.wait_ge(dve_early.sem, dve_early.next(b, ahead, n))

            def early_ln(b, ahead):
                ve.wait_ge(x_landed.sem, x_landed.next(b, ahead, 16))
                carry(ve)
                for t in range(NT):
                    ins = ve.bn_stats(early_stats[:, t, :], xin[:, t, :])
                early_link(b, ahead, 1, ins)
                carry(ve)
                for t in range(NT):
                    ins = ve.bn_aggr(early_mv[:, t, :], early_stats[:, t, :])
                early_link(b, ahead, 2, ins)
                ln_var.by(ve.tensor_scalar(early_mv[:, :, 1], early_mv[:, :, 1], EPS_LN, None, ALU.add))

            def early_coef(b, ahead):
                ve.wait_ge(ln_rstd.sem, ln_rstd.next(b, ahead, 1))
                ln_coef.by(ve.scalar_tensor_tensor(early_shift[:, :], early_mv[:, :, 0], -1.0, early_rstd[:, :],
                                                   ALU.mult, ALU.mult))

            def early_values(b, ahead):
                ve.wait_ge(v_ps.sem, v_ps.next(b, ahead, 1))
                bv = brow[:, BV:BV + 1, :].broadcast_to([P, NT, D]).rearrange("p t (h f) -> p t h f", h=H0)
                v_ready.by(ve.tensor_tensor(
                    v0[:, :, :, :], ps[:, 4:6, :].rearrange("p a (t h f) -> p (a t) h f", h=H0, f=DH0), bv,
                    ALU.add))

            def early_low_parts(b, ahead, u):
                ve.wait_ge(part_h.sem, part_h.next(b, ahead, u + 1))
                ve.wait_ge(qk_ps.sem, qk_ps.next(b, ahead, 2))
                acc = ps[:, 2 * u:2 * u + 2, :].rearrange("p a n -> p (a n)")
                early_link(b, ahead, 3 + 2 * u, ve.scalar_tensor_tensor(
                    resid0[u], acc, bcol[:, u:u + 1], parts[:, u, 0, :], ALU.add, ALU.subtract))
                early_link(b, ahead, 4 + 2 * u, ve.tensor_copy(parts[:, u, 1, :], resid0[u]))
                parts_ready.by(ve.tensor_tensor(parts[:, u, 2, :], resid0[u], parts[:, u, 1, :], ALU.subtract))

            def batch(b, last):
                chain[0] = 0

                def link(ins):
                    chain[0] += 1
                    dve.by(ins)
                    ve.wait_ge(dve.sem, dve.at(b, chain[0]))

                def mark(ins):
                    chain[0] += 1
                    dve.by(ins)
                    return chain[0]

                def after(count):
                    ve.wait_ge(dve.sem, dve.at(b, count))

                def ln_sums(src, ready):
                    tiles = [range(g * HT, (g + 1) * HT) for g in range(2)]
                    spans = [slice(g * HT, (g + 1) * HT) for g in range(2)]
                    sampled, averaged = [], []
                    for g in range(2):
                        ready(g)
                        carry(ve)
                        for t in tiles[g]:
                            ins = ve.bn_stats(stats[:, t, :], src[:, t, :])
                        sampled.append(mark(ins))
                    for g in range(2):
                        after(sampled[g])
                        carry(ve)
                        for t in tiles[g]:
                            ins = ve.bn_aggr(mv[:, t, :], stats[:, t, :])
                        averaged.append(mark(ins))
                    for g in range(2):
                        after(averaged[g])
                        ln_var.by(ve.tensor_scalar(mv[:, spans[g], 1], mv[:, spans[g], 1], EPS_LN, None, ALU.add))
                    return averaged

                def ln(src, k, c, ready):
                    ln_sums(src, ready)
                    for g in range(2):
                        tiles = slice(g * HT, (g + 1) * HT)
                        ve.wait_ge(ln_rstd.sem, ln_rstd.at(b, 2 * k + g))
                        ln_coef.by(ve.scalar_tensor_tensor(shift[:, tiles], mv[:, tiles, 0], -1.0,
                                                           rstd[:, tiles], ALU.mult, ALU.mult))

                def ln_affine(src, k, ready, gamma, plus, dst, done, before=None):
                    averaged = ln_sums(src, ready)
                    scaled = []
                    for g in range(2):
                        after(averaged[g])
                        for t in range(g * HT, (g + 1) * HT):
                            ins = ve.scalar_tensor_tensor(bufd[:, t, :], src[:, t, :], mv[:, t, 0:1],
                                                          brow[:, gamma, :], ALU.subtract, ALU.mult)
                        scaled.append(mark(ins))
                    if before:
                        before()
                    for g in range(2):
                        ve.wait_ge(ln_rstd.sem, ln_rstd.at(b, 2 * k + g))
                        after(scaled[g])
                        for t in range(g * HT, (g + 1) * HT):
                            ins = ve.scalar_tensor_tensor(dst[:, t, :], bufd[:, t, :], rstd[:, t:t + 1], plus(t),
                                                          ALU.mult, ALU.add)
                        done(ins)

                def low_parts():
                    for u in range(2):
                        ve.wait_ge(part_h.sem, part_h.at(b, 2 + u + 1))
                        acc = ps[:, 2 * u:2 * u + 2, :].rearrange("p a n -> p (a n)")
                        link(ve.tensor_tensor(resid[:, u, :], acc, parts[:, u, 0, :], ALU.subtract))
                        link(ve.tensor_copy(parts[:, u, 1, :], resid[:, u, :]))
                        parts_ready.by(ve.tensor_tensor(parts[:, u, 2, :], resid[:, u, :], parts[:, u, 1, :],
                                                        ALU.subtract))

                def gat_out_of_psum(nh, f, v, cat):
                    for g in range(3):
                        k = min(3, NT - 3 * g)
                        acc = ps[:, g, 0:k * cat].rearrange("p (t c) -> p t c", c=cat)
                        ve.tensor_copy(v[:, 3 * g:3 * g + k, :, 0:f - 1],
                                       acc[:, :, 0:D].rearrange("p t (h f) -> p t h f", h=nh))
                        ins = ve.tensor_copy(sd[:, 3 * g:3 * g + k, 0:2 * nh], acc[:, :, D:D + 2 * nh])
                    lin_out.by(ins)

                def gat_weights(nh, which):
                    s, d = sd[:, :, 0:nh], sd[:, :, nh:2 * nh]
                    ve.wait_ge(lin_out.sem, lin_out.at(b, which + 1))
                    top1.by(ve.tensor_reduce(dmx[:, 0:nh], d.rearrange("p t h -> p h t"), AX.X, ALU.max))
                    ve.wait_ge(top1T.sem, top1T.at(b, which + 1))
                    link(ve.tensor_reduce(dmc[0:nh, :], ps[0:nh, 6, 0:P], AX.X, ALU.max))
                    top_diag.by(ve.tensor_scalar(dmdiag[0:nh, 0:nh], ident[0:nh, 0:nh], dmc[0:nh, 0:1], None,
                                                 ALU.mult))
                    ve.wait_ge(top_ps.sem, top_ps.at(b, which + 1))
                    link(ve.tensor_copy(dmax[:, 0:nh], ps[:, 7, 0:nh]))
                    top = dmax[:, 0:nh].unsqueeze(1).broadcast_to([P, NT, nh])
                    u, m = tm[:, 0, :, 0:nh], tm[:, 1, :, 0:nh]
                    link(ve.tensor_tensor(arg[:, 2, :, 0:nh], d, top, ALU.subtract))
                    link(ve.tensor_tensor(u, s, top, ALU.add))
                    link(ve.tensor_scalar(arg[:, 3, :, 0:nh], arg[:, 2, :, 0:nh], SLOPE, None, ALU.mult))
                    link(ve.scalar_tensor_tensor(m, u, SLOPE, u, ALU.mult, ALU.max))
                    if which == 0:
                        link(ve.tensor_scalar(m, m, bcol[:, 3:4], None, ALU.add))
                        link(ve.scalar_tensor_tensor(arg[:, 0, :, 0:nh], u, bcol[:, 3:4], m, ALU.add,
                                                     ALU.subtract))
                        link(ve.tensor_scalar(u, u, SLOPE, bcol[:, 3:4], ALU.mult, ALU.add))
                        args_ready.by(ve.tensor_tensor(arg[:, 1, :, 0:nh], u, m, ALU.subtract))
                    else:
                        link(ve.tensor_tensor(arg[:, 0, :, 0:nh], u, m, ALU.subtract))
                        args_ready.by(ve.scalar_tensor_tensor(arg[:, 1, :, 0:nh], u, SLOPE, m, ALU.mult,
                                                              ALU.subtract))

                def split_high(nh, f, r, src, which):
                    ve.wait_ge(weights.sem, weights.at(b, which + 1))
                    va, _, _ = gat_views(nh, f)
                    wa = ew[:, 2, :, 0:nh].unsqueeze(3).broadcast_to([P, NT, nh, f])
                    link(ve.tensor_scalar(tm[:, 0, :, 0:nh], sd[:, :, nh:2 * nh], -1.0, None, ALU.mult))
                    link(ve.tensor_tensor(va, src, wa, ALU.mult))
                    link(ve.tensor_copy(r[:, :, :, 0, 0, :], va))
                    link(ve.tensor_tensor(va, va, r[:, :, :, 0, 0, :], ALU.subtract))
                    link(ve.tensor_copy(r[:, :, :, 0, 1, :], va))
                    ra_ready.by(ve.tensor_tensor(r[:, :, :, 0, 2, :], va, r[:, :, :, 0, 1, :], ALU.subtract))

                def split_rest(nh, f, r, src):
                    k = NT - POOL_SPLIT
                    vb, r, src = gat_views(nh, f)[1][:, POOL_SPLIT:], r[:, POOL_SPLIT:], src[:, POOL_SPLIT:]
                    wb = ew[:, 3, POOL_SPLIT:, 0:nh].unsqueeze(3).broadcast_to([P, k, nh, f])
                    link(ve.tensor_tensor(vb, src, wb, ALU.mult))
                    link(ve.tensor_copy(r[:, :, :, 1, 0, :], vb))
                    link(ve.tensor_tensor(vb, vb, r[:, :, :, 1, 0, :], ALU.subtract))
                    link(ve.tensor_copy(r[:, :, :, 1, 1, :], vb))
                    rb_ready.by(ve.tensor_tensor(r[:, :, :, 1, 2, :], vb, r[:, :, :, 1, 1, :], ALU.subtract))

                def steps(n, h, src):
                    for jt in range(NT):
                        k = n * NT + jt
                        if 8 <= k < NT * H1:
                            ve.wait_ge(step_used.sem, step_used.at(b, k - 7))
                        if jt < ACT_TILES:
                            m = n * ACT_TILES + jt
                            ve.wait_ge(sign_ready.sem, sign_ready.at(b, m + 1))
                            step_ready.by(ve.tensor_tensor(step[:, k % 8, :], sign[:, m % 4, :],
                                                           block_t[:, jt, :], ALU.is_gt))
                        else:
                            step_ready.by(ve.scalar_tensor_tensor(step[:, k % 8, :], src, tm[:, 0, jt, h:h + 1],
                                                                  mask_t[:, jt, :], ALU.is_gt, ALU.mult))

                def invert(c):
                    ve.wait_ge(den0.sem, den0.at(b, c + 1))
                    link(ve.transpose(den_t, ps[:, 6 + c % 2, :]))
                    return mark(ve.reciprocal(rden[:, 0:32].rearrange("p (a k) -> p a k", a=2),
                                       den_t.rearrange("p (k a r) -> p a k r", a=2, r=DH0 // 2)[:, :, :, 0]))

                def spread(c, inverted):
                    after(inverted)
                    if c == 2:
                        ve.wait_ge(share0.sem, share0.at(b, 1))
                    if c >= 3:
                        ve.wait_ge(ctx0.sem, ctx0.at(b, c - 2))
                    carry(ve)
                    inv_ready.by(ve.transpose(inv0[c % 2].rearrange("p (k r) -> p k r", r=32),
                                              rden[:, 0:32].unsqueeze(2).broadcast_to([P, 32, 32])))

                for n in range(H0 * NT):
                    c, h = n // H0, n % H0
                    ve.wait_ge(s0_ready.sem, s0_ready.at(b, n + 1))
                    if c >= 2:
                        ve.wait_ge(pv0.sem, pv0.at(b, c - 1))
                    clip_ready.by(ve.scalar_tensor_tensor(
                        maps[:, n % 8, :], ps[:, 2 * (n % 2):2 * (n % 2) + 2, :].rearrange("p a n -> p (a n)"),
                        -CLIP, limit_t[:, c, :], ALU.max, ALU.min))
                    if c and h == 1:
                        inverted = invert(c - 1)
                    if c and h == 2:
                        spread(c - 1, inverted)
                spread(NT - 1, invert(NT - 1))
                last_inv, total = inv0[(NT - 1) % 2], flat(bufc[:, :, :])
                ve.wait_ge(inv_ready.sem, inv_ready.at(b, NT))
                ve.wait_ge(pv0.sem, pv0.at(b, NT))
                halves = [slice(g * HALF, (g + 1) * HALF) for g in range(2)]
                marks = [mark(ve.tensor_tensor(last_inv[:, halves[g]], ps[:, 4 + g, :], last_inv[:, halves[g]],
                                               ALU.mult)) for g in range(2)]
                ve.wait_ge(ctx0.sem, ctx0.at(b, NT - 2))
                for g in range(2):
                    after(marks[g])
                    ctx0_done.by(ve.tensor_tensor(total[:, halves[g]], total[:, halves[g]],
                                                  last_inv[:, halves[g]], ALU.add))
                ve.wait_ge(plus_row.sem, plus_row.at(b, 2))
                summed = []
                for g in range(2):
                    ve.wait_ge(lin_ps.sem, lin_ps.at(b, WO_PS + g + 1))
                    summed.append(mark(ve.tensor_tensor(half_of(bufc, g), acc_half(4 + g), half_of(hn, g), ALU.add)))
                ln_affine(bufc, 1, lambda g: after(summed[g]), GAMMA, lambda t: xin[:, t, :], xr, x_freed.by,
                          lambda: ve.wait_ge(x_stored.sem, x_stored.at(b, 0)))

                ln(xr, 2, 0, lambda g: ve.wait_ge(x_freed.sem, x_freed.at(b, g + 1)))
                ve.wait_ge(lin_ps.sem, lin_ps.at(b, IN1_PS + 1))
                ve.tensor_copy(v1[:, :, :, DH1], ones[:, 0:NT * H1].rearrange("p (t h) -> p t h", h=H1))
                gat_out_of_psum(H1, F1, v1, D + 2 * H1)
                gat_weights(H1, 0)
                split_high(H1, F1, r1, v1[:, :, :, :], 0)
                split_rest(H1, F1, r1, v1[:, :, :, :])
                ve.wait_ge(csum_ps.sem, csum_ps.at(b, 1))
                csum_out.by(ve.tensor_copy(csum[:, :], ps[:, 7, 0:H1 * F1]))

                def g_sums():
                    for it in range(NT):
                        ve.wait_ge(g_ps.sem, g_ps.at(b, it + 1))
                        acc = ps[:, 4 + it % 4, 0:H1 * 3 * F1].rearrange("p (h r f) -> p h f r", h=H1, r=3)
                        g_out.by(ve.tensor_reduce(gsum[:, it, :, :], acc, AX.X, ALU.add))

                def t_sums(h):
                    _, _, ts = gat_views(H1, F1)
                    ve.wait_ge(step_used.sem, step_used.at(b, NT * (h + 1)))
                    for half in range(2):
                        acc = ps[:, 4 + 2 * (h % 2) + half, 0:4 * 6 * F1].rearrange(
                            "p (t s r f) -> p t s f r", t=4, s=2, r=3)
                        ins = ve.tensor_reduce(ts[:, 4 * half:4 * half + 4, h, :, :], acc, AX.X, ALU.add)
                    t_out.by(ins)

                ve.wait_ge(rb_ready.sem, rb_ready.at(b, 2))
                for h in range(H1):
                    ve.wait_ge(rows_out.sem, rows_out.at(b, h + 1))
                    steps(h, h, sbc[:, h % 2, :])
                    if h == 0:
                        g_sums()
                    else:
                        t_sums(h - 1)
                t_sums(H1 - 1)
                ve.wait_ge(mixed.sem, mixed.at(b, H1))
                ta = gat_views(H1, F1)[2][:, :, :, 0, :]
                rd = rden[:, :].rearrange("p (t h) -> p t h", h=H1)
                marks = [mark(ve.reciprocal(half_of(rd, g), ta[:, g * HT:(g + 1) * HT, :, DH1])) for g in range(2)]
                for g in range(2):
                    after(marks[g])
                    hn1_ready.by(ve.tensor_tensor(
                        half_of(bufc, g).rearrange("p t (h f) -> p t h f", h=H1),
                        ta[:, g * HT:(g + 1) * HT, :, 0:DH1],
                        half_of(rd, g).unsqueeze(3).broadcast_to([P, HT, H1, DH1]), ALU.mult))
                summed = []
                for g in range(2):
                    ve.wait_ge(lin_ps.sem, lin_ps.at(b, OUT1_PS + g + 1))
                    summed.append(mark(ve.tensor_tensor(half_of(xr, g), acc_half(4 + g), half_of(xr, g), ALU.add)))

                ln(xr, 3, 1, lambda g: after(summed[g]))
                low_parts()
                ve.wait_ge(v_ps.sem, v_ps.at(b, 2))
                v_ready.by(ve.tensor_copy(v2[:, :, :, 0:DH1],
                                          ps[:, 4:6, :].rearrange("p a (t h f) -> p (a t) h f", h=H1, f=DH1)))

                def row_max(h, a):
                    it, half = a // 2, a % 2
                    n = h * 2 * NT + a
                    ve.wait_ge(nat_ps.sem, nat_ps.at(b, n + 1))
                    if n >= 3:
                        ve.wait_ge(nat_used.sem, nat_used.at(b, n - 2))
                    carry(ve)
                    nat_used.by(ve.tensor_tensor_reduce(
                        junk[:, n % 3, :], ps[:, 6 + n % 2, :], block_n[:, it, half * HALF:(half + 1) * HALF],
                        1.0, -3.0e38, ALU.add, ALU.max, msplit[:, h % 2, it, half:half + 1]))

                def minus_max(h):
                    ve.wait_ge(nat_used.sem, nat_used.at(b, (h + 1) * 2 * NT))
                    if h >= 2:
                        ve.wait_ge(mrow_ps.sem, mrow_ps.at(b, h - 1))
                    link(ve.tensor_tensor(mtop[:, h % 2, :], msplit[:, h % 2, :, 0], msplit[:, h % 2, :, 1],
                                          ALU.max))
                    mneg_ready.by(ve.tensor_scalar(mneg[:, h % 2, :], mtop[:, h % 2, :], -1.0, None, ALU.mult))

                def context(q):
                    ve.wait_ge(turned.sem, turned.at(b, 8 + 2 * q + 2))
                    for e in range(2):
                        acc = ps[:, 6 + e, :].rearrange("p (k c s f) -> p s k f c", k=4, c=2, s=2)
                        for half in range(2):
                            ins = ve.tensor_reduce(gsum[:, 4 * half:4 * half + 4, 2 * q + e, :],
                                                   acc[:, half, :, 0:F1, :], AX.X, ALU.add)
                    ctx2_nat.by(ins)

                for a in range(2 * NT):
                    row_max(0, a)
                minus_max(0)
                for h in range(H1):
                    a = 0
                    for jt in range(NT):
                        if h + 1 < H1:
                            for _ in range(AHEAD[jt]):
                                row_max(h + 1, a)
                                a += 1
                            if AHEAD[jt] and a == 2 * NT:
                                minus_max(h + 1)
                        if h == H1 - 1 and jt % 2 and jt < NT - 1:
                            context(jt // 2)

                context(H1 // 2 - 1)
                ve.wait_ge(ctx2_nat.sem, ctx2_nat.at(b, H1 // 2))
                rd = rden[:, :].rearrange("p (t h) -> p t h", h=H1)
                marks = [mark(ve.reciprocal(half_of(rd, g), gsum[:, g * HT:(g + 1) * HT, :, DH1]))
                         for g in range(2)]
                for g in range(2):
                    after(marks[g])
                    marks[g] = mark(ve.tensor_tensor(
                        half_of(bufc, g).rearrange("p t (h f) -> p t h f", h=H1),
                        gsum[:, g * HT:(g + 1) * HT, :, 0:DH1],
                        half_of(rd, g).unsqueeze(3).broadcast_to([P, HT, H1, DH1]), ALU.mult))
                for g in range(2):
                    after(marks[g])
                    marks[g] = mark(ve.tensor_tensor(half_of(bufc, g), half_of(bufc, g), half_of(hn, g), ALU.add))
                ln_affine(bufc, 4, lambda g: after(marks[g]), G1, lambda t: brow[:, BE1, :], bufc, x1_ready.by)
                ve.wait_ge(plus_row.sem, plus_row.at(b, 4))
                for g in range(2):
                    ve.wait_ge(lin_ps.sem, lin_ps.at(b, FFN2_PS + g + 1))
                    marks[g] = mark(ve.tensor_tensor(half_of(bufc, g), acc_half(2 + g), half_of(hn, g), ALU.add))
                final = []
                ln_affine(bufc, 5, lambda g: after(marks[g]), G2, lambda t: xr[:, t, :], xr,
                          lambda ins: final.append(mark(ins)))

                ln(xr, 6, 2, lambda g: after(final[g]))
                if not last:
                    early_ln(b, 1)
                    early_coef(b, 1)
                ve.wait_ge(lin_ps.sem, lin_ps.at(b, IN3_PS + 1))
                gat_out_of_psum(1, F3, v3, D + 2)
                gat_weights(1, 1)
                ve.wait_ge(csum_ps.sem, csum_ps.at(b, 2))
                csum_out.by(ve.tensor_copy(csum[:, 0:F3], ps[:, 3, 0:F3]))
                split_high(1, F3, r3, v3[:, :, :, :], 1)
                if not last:
                    early_values(b, 1)
                ve.wait_ge(rows_out.sem, rows_out.at(b, H1 + 1))
                steps(H1, 0, flat(bufd[:, :, :]))
                ve.wait_ge(step_ready.sem, step_ready.at(b, NT * (H1 + 1)))
                for jt in range(NT):
                    rest_ready.by(ve.tensor_tensor(rest[:, jt, :], mask_t[:, jt, :], step[:, jt, :],
                                                   ALU.subtract))
                if not last:
                    early_low_parts(b, 1, 0)
                ve.wait_ge(csum_out.sem, csum_out.at(b, 2))
                for it in range(NT):
                    ta, tb = t3s[:, it % 2, 0, :], t3s[:, it % 2, 1, :]
                    ve.wait_ge(t3_ps.sem, t3_ps.at(b, it + 1))
                    for s in range(2):
                        acc = ps[:, 4 + 2 * (it % 2) + s, 0:3 * F3].rearrange("p (r f) -> p f r", r=3)
                        ins = ve.tensor_reduce(t3s[:, it % 2, s, :], acc, AX.X, ALU.add)
                    t3_out.by(ins)
                    ve.wait_ge(t3_out.sem, t3_out.at(b, it + 1))
                    link(ve.tensor_scalar(ta, ta, ew[:, 0, it, 0:1], None, ALU.mult))
                    link(ve.scalar_tensor_tensor(ta, tb, ew[:, 1, it, 0:1], ta, ALU.mult, ALU.add))
                    link(ve.scalar_tensor_tensor(ta, csum[:, 0:F3], empty[:, it:it + 1], ta, ALU.mult, ALU.add))
                    link(ve.reciprocal(rden[:, it:it + 1], t3s[:, it % 2, 0, D:F3]))
                    link(ve.tensor_scalar(bufd[:, it, :], t3s[:, it % 2, 0, 0:D], rden[:, it:it + 1], None,
                                          ALU.mult))
                    if it == 1 and not last:
                        early_low_parts(b, 1, 1)
                    if it % HT == HT - 1:
                        g = it // HT
                        elu_ready.by(ve.tensor_scalar(half_of(bufc, g), half_of(bufd, g), 0.0, None, ALU.min))
                        link(ve.tensor_scalar(half_of(bufd, g), half_of(bufd, g), 0.0, -1.0, ALU.max, ALU.add))
                        link(ve.tensor_tensor(half_of(xr, g), half_of(xr, g), half_of(bufd, g), ALU.add))
                for g in range(2):
                    ve.wait_ge(elu_exp.sem, elu_exp.at(b, g + 1))
                    x_done.by(ve.tensor_tensor(half_of(xr, g), half_of(xr, g), half_of(bufc, g), ALU.add))
                assert chain[0] == dve.per, ("DVE_CHAIN", chain[0])

            early_ln(0, 0)
            early_coef(0, 0)
            early_values(0, 0)
            early_low_parts(0, 0, 0)
            early_low_parts(0, 0, 1)
            if B > 1:
                with ve.Fori(0, B - 1) as b:
                    batch(b, False)
            batch(B - 1, True)

        @block.tensor
        def _(pe):
            pe.wait_ge(loaded.sem, 16 * len(LOADS))
            pe.wait_ge(set_pool.sem, 13)
            for n in range(5):
                ins = pe.transpose(ps[:, n // 4, (n % 4) * D:(n % 4 + 1) * D], raw_w[:, n, :], ident[:, :])
            ins.then_inc(set_pe.sem, 1)
            pe.wait_ge(set_dve.sem, setup_marks["nat"])
            for jt in range(NT):
                if jt >= 2:
                    pe.wait_ge(set_dve.sem, setup_marks["turn"] - NT + jt - 1)
                bank = ps[:, 2 + jt % 2, :].bitcast(BF16)
                for it in range(NT):
                    ins = pe.transpose(bank[:, it * P:(it + 1) * P], nat01[:, it, jt * P:(jt + 1) * P],
                                       ident_b[:, :])
                ins.then_inc(set_pe.sem, 1)
            pe.wait_ge(set_dve.sem, setup_marks["end"])

            def early_turn(b, ahead):
                for t in range(NT):
                    pe.wait_ge(h_tile.sem, h_tile.next(b, ahead, t + 1))
                    ins = pe.transpose(ps[:, 6 + t // 4, (t % 4) * P:(t % 4 + 1) * P], hn[:, t, :], ident[:, :])
                    if t % 4 == 3:
                        turned.by(ins)

            def early_projections(b, ahead):
                pe.wait_ge(actT.sem, actT.next(b, ahead, 2))
                for t in range(NT):
                    ins = pe.matmul(ps[:, 4 + t // 4, (t % 4) * D:(t % 4 + 1) * D], hT[:, t * P:(t + 1) * P],
                                    wT[:, 2, :], start=True, stop=True)
                v_ps.by(ins)
                for u in range(2):
                    if ahead:
                        if u == 0:
                            pe.wait_ge(rows_out.sem, rows_out.at(b, H1 + 1))
                        else:
                            pe.wait_ge(csum_out.sem, csum_out.at(b, 2))
                    for half in range(2):
                        ins = pe.matmul(ps[:, 2 * u + half, :], wT[:, u, :], hT[:, half * HALF:(half + 1) * HALF],
                                        start=True, stop=True)
                    qk_ps.by(ins)

            def batch(b, last):
                def turn(src, event):
                    for t in range(NT):
                        if callable(event):
                            event(t)
                        ins = pe.transpose(ps[:, 6 + t // 4, (t % 4) * P:(t % 4 + 1) * P], src(t), ident[:, :])
                        if t % 4 == 3:
                            turned.by(ins)

                def turn_h(m):
                    turn(lambda t: hn[:, t, :], lambda t: pe.wait_ge(h_tile.sem, h_tile.at(b, m * NT + t + 1)))

                def project(bank, lhsT, rhs=hT):
                    for half in range(2):
                        ins = pe.matmul(ps[:, bank + half, :], lhsT, rhs[:, half * HALF:(half + 1) * HALF],
                                        start=True, stop=True)
                    return ins

                def rows_of(src, rhs, bank, width, per_bank, ready=None, signal_half=None):
                    for t in range(NT):
                        if ready and t % HT == 0:
                            ready(t // HT)
                        at = (t % per_bank) * width
                        ins = pe.matmul(ps[:, bank + t // per_bank, at:at + width], src[:, t * P:(t + 1) * P],
                                        rhs, start=True, stop=True)
                        if signal_half and t % HT == HT - 1:
                            signal_half.by(ins)
                    return ins

                def turned_out(n):
                    return lambda g: pe.wait_ge(actT.sem, actT.at(b, 2 * n + g + 1))

                def top_across(nh, which):
                    pe.wait_ge(top1.sem, top1.at(b, which + 1))
                    top1T.by(pe.transpose(ps[0:nh, 6, 0:P], dmx[:, 0:nh], ident[:, :]))
                    pe.wait_ge(top_diag.sem, top_diag.at(b, which + 1))
                    top_ps.by(pe.matmul(ps[:, 7, 0:nh], ones[0:nh, 0:P], dmdiag[0:nh, 0:nh], start=True, stop=True))

                pe.wait_ge(parts_ready.sem, parts_ready.at(b, 2))
                pe.wait_ge(v_ready.sem, v_ready.at(b, 1))

                def scores0(n):
                    c, h = n // H0, n % H0
                    if c == 0:
                        pe.wait_ge(stack[h].sem, stack[h].at(b, 32 * len(TERMS0[0])))
                    if n >= 2:
                        pe.wait_ge(clip_ready.sem, clip_ready.at(b, n - 1))
                    for half in range(2):
                        for s in range(2):
                            ins = pe.matmul(ps[:, 2 * (n % 2) + half, :],
                                            stk[0:K0[s], 2 * h + s, c * P:(c + 1) * P],
                                            stq[0:K0[s], 2 * h + s, half * HALF:(half + 1) * HALF],
                                            start=(s == 0), stop=(s == 1))
                    s0_ready.by(ins)

                def denominators0(c, half):
                    if half == 0:
                        pe.wait_ge(p0_ready.sem, p0_ready.at(b, H0 * (c + 1)))
                        if c >= 2:
                            pe.wait_ge(inv_ready.sem, inv_ready.at(b, c - 1))
                    for h in range(H0):
                        ins = pe.matmul(ps[DH0 * h:DH0 * (h + 1), 6 + c % 2, :], pick[:, half, :],
                                        maps[:, (H0 * c + h) % 8, half * HALF:(half + 1) * HALF],
                                        start=(half == 0), stop=(half == 1))
                    if half:
                        den0.by(ins)

                def values0(c, half):
                    if c and half == 0:
                        pe.wait_ge(sums0.sem, sums0.at(b, c))
                    for h in range(H0):
                        ins = pe.matmul(ps[DH0 * h:DH0 * (h + 1), 4 + half, :], v0[:, c, h, :],
                                        maps[:, (H0 * c + h) % 8, half * HALF:(half + 1) * HALF],
                                        start=True, stop=True)
                    if half:
                        pv0.by(ins)

                for n in range(H0):
                    scores0(n)
                for c in range(NT):
                    for k in range(H0):
                        if c + 1 < NT:
                            scores0(H0 * (c + 1) + k)
                        (denominators0, values0)[k // 2](c, k % 2)
                pe.wait_ge(ctx0_done.sem, ctx0_done.at(b, 1))
                rows_of(flat(bufc[:, :, :]), wT[:, 3, :], 4, D, 4,
                        lambda g: pe.wait_ge(ctx0_done.sem, ctx0_done.at(b, g + 1)), lin_ps)

                turn_h(1)
                lin_ps.by(rows_of(hT, w1cat[:, :], 0, D + 2 * H1, 3, turned_out(1)))
                pe.wait_ge(lin_out.sem, lin_out.at(b, 1))

                def s_rows(n, cat, at, bank):
                    rows_ps.by(project(bank, cat[:, at:at + 1].broadcast_to([P, P])))

                s_rows(0, w1cat, D, 0)
                s_rows(1, w1cat, D + 1, 2)
                top_across(H1, 0)
                pe.wait_ge(args_ready.sem, args_ready.at(b, 1))
                for t in range(NT):
                    ins = pe.matmul(ps[:, 7, 0:H1 * F1], ones[:, 0:P], v1[:, t, :, :].rearrange("p h f -> p (h f)"),
                                    start=(t == 0), stop=(t == NT - 1))
                csum_ps.by(ins)
                pe.wait_ge(rb_ready.sem, rb_ready.at(b, 2))
                pe.wait_ge(ra_ready.sem, ra_ready.at(b, 1))
                pe.wait_ge(csum_out.sem, csum_out.at(b, 1))
                for it in range(NT):
                    if it >= 4:
                        pe.wait_ge(g_out.sem, g_out.at(b, it - 3))
                    for jt in range(NT):
                        ins = pe.matmul(ps[:, 4 + it % 4, 0:H1 * 3 * F1], mask_t[:, jt, it * P:(it + 1) * P],
                                        r1[:, jt, :, 1, :, :].rearrange("p h r f -> p h (r f)"),
                                        start=(jt == 0), stop=(jt == NT - 1))
                    g_ps.by(ins)
                for h in range(H1):
                    if h == 0:
                        pe.wait_ge(g_out.sem, g_out.at(b, NT))
                    if h >= 2:
                        pe.wait_ge(t_out.sem, t_out.at(b, h - 1))
                    for jt in range(NT):
                        k = h * NT + jt
                        pe.wait_ge(step_ready.sem, step_ready.at(b, k + 1))
                        for it in range(NT):
                            at = (it % 4) * 6 * F1
                            ins = pe.matmul(ps[:, 4 + 2 * (h % 2) + it // 4, at:at + 6 * F1],
                                            step[:, k % 8, it * P:(it + 1) * P],
                                            r1[:, jt, h, :, :, :].rearrange("p s r f -> p (s r f)"),
                                            start=(jt == 0 and it % 4 == 0), stop=(jt == NT - 1),
                                            skip_group_check=True)
                        step_used.by(ins)
                    if h + 2 < H1:
                        pe.wait_ge(rows_out.sem, rows_out.at(b, h + 1))
                        s_rows(h + 2, w1cat, D + h + 2, 2 * (h % 2))
                turn(lambda t: bufc[:, t, :],
                     lambda t: t % HT or pe.wait_ge(hn1_ready.sem, hn1_ready.at(b, t // HT + 1)))
                pe.wait_ge(t_out.sem, t_out.at(b, H1))
                rows_of(flat(bufd[:, :, :]), wT[:, 4, :], 4, D, 4, turned_out(2), lin_ps)

                turn_h(2)
                pe.wait_ge(actT.sem, actT.at(b, 8))
                qk_ps.by(project(0, wqkv[:, 0:D]))
                qk_ps.by(project(2, wqkv[:, D:2 * D]))
                v_ps.by(rows_of(hT, wqkv[:, 2 * D:3 * D], 4, D, 4))
                pe.wait_ge(parts_ready.sem, parts_ready.at(b, 4))
                pe.wait_ge(v_ready.sem, v_ready.at(b, 2))
                pe.wait_ge(ones_row.sem, ones_row.at(b, 16))

                def natural_scores(h, a):
                    n = h * 2 * NT + a
                    it, half = a // 2, a % 2
                    if a == 0:
                        pe.wait_ge(stack[h].sem, stack[h].at(
                            b, 32 * len(TERMS2) + (32 * len(TERMS0[0]) if h < H0 else 0)))
                        if h:
                            pe.wait_ge(mrow_ready.sem, mrow_ready.at(b, h))
                    if n >= 2:
                        pe.wait_ge(nat_used.sem, nat_used.at(b, n - 1))
                    nat_ps.by(pe.matmul(ps[:, 6 + n % 2, :], stq[0:K2, h, it * P:(it + 1) * P],
                                        stk[0:K2, h, half * HALF:(half + 1) * HALF], start=True, stop=True))

                def max_row(h):
                    pe.wait_ge(mneg_ready.sem, mneg_ready.at(b, h + 1))
                    for it in range(NT):
                        ins = pe.matmul(ps[K2:K2 + 1, 6 + it // 4, (it % 4) * P:(it % 4 + 1) * P],
                                        mneg[:, h % 2, it:it + 1], ident_b[:, :], start=True, stop=True)
                    mrow_ps.by(ins)

                def scores2(n, half):
                    h, jt = n // NT, n % NT
                    if jt == 0:
                        pe.wait_ge(mrow_ready.sem, mrow_ready.at(b, h + 1))
                    if n >= 2:
                        pe.wait_ge(p2_ready.sem, p2_ready.at(b, n - 1))
                    cols = slice(half * HALF, (half + 1) * HALF)
                    pe.matmul(ps[:, 2 * (n % 2) + half, :], stk[0:K2 + 1, h, jt * P:(jt + 1) * P],
                              stq[0:K2 + 1, h, cols], start=True, stop=False)
                    ins = pe.matmul(ps[:, 2 * (n % 2) + half, :], neg_ident_b[:, :], block_t[:, jt, cols],
                                    start=False, stop=True)
                    if half:
                        s2_ready.by(ins)

                def values2(m):
                    h, jt = m // 4, 2 * (m % 4)
                    pe.wait_ge(p2_ready.sem, p2_ready.at(b, 2 * m + 2))
                    if m % 4 == 0 and h >= 2:
                        pe.wait_ge(ctx2_out.sem, ctx2_out.at(b, h - 1))
                    for odd in range(2):
                        for half in range(2):
                            c = 32 * (2 * odd + half)
                            ins = pe.matmul(ps[c:c + 32, 4 + h % 2, :], v2[:, jt + odd, h, :],
                                            maps[:, (2 * m + odd) % 4, half * HALF:(half + 1) * HALF],
                                            start=(m % 4 == 0), stop=(m % 4 == 3))
                    pv2.by(ins)

                for a in range(2 * NT):
                    natural_scores(0, a)
                max_row(0)
                scores2(0, 0)
                scores2(0, 1)

                def turn_context(q):
                    pe.wait_ge(ctx2_out.sem, ctx2_out.at(b, 2 * q + 2))
                    if q == 0:
                        pe.wait_ge(mrow_ready.sem, mrow_ready.at(b, H1))
                    else:
                        pe.wait_ge(ctx2_nat.sem, ctx2_nat.at(b, q))
                    for e in range(2):
                        for k in range(4):
                            ins = pe.transpose(ps[:, 6 + e, k * P:(k + 1) * P],
                                               ctx2[:, 2 * q + e, k * P:(k + 1) * P], ident[:, :])
                        turned.by(ins)

                for h in range(H1):
                    a = 0
                    for jt in range(NT):
                        n = h * NT + jt
                        left = AHEAD[jt] if h + 1 < H1 else 0
                        for half in range(2):
                            if left > half:
                                natural_scores(h + 1, a)
                                a += 1
                            if n + 1 < H1 * NT:
                                scores2(n + 1, half)
                        for _ in range(2, left):
                            natural_scores(h + 1, a)
                            a += 1
                        if jt % 2:
                            values2(n // 2)
                            if h == H1 - 1 and jt < NT - 1:
                                turn_context(jt // 2)
                        if jt == NT - 3 and h + 1 < H1:
                            max_row(h + 1)
                turn_context(H1 // 2 - 1)
                turn(lambda t: bufc[:, t, :],
                     lambda t: t % HT or pe.wait_ge(x1_ready.sem, x1_ready.at(b, t // HT + 1)))
                for half in range(2):
                    turned_out(4)(half)
                    lin_ps.by(pe.matmul(ps[:, half, :], ffn1[:, :], hT[:, half * HALF:(half + 1) * HALF],
                                        start=True, stop=True))
                rows_of(flat(bufd[:, :, :]), ffn2[:, :], 2, D, 4,
                        lambda g: pe.wait_ge(z_out.sem, z_out.at(b, g + 1)), lin_ps)

                turn_h(3)
                lin_ps.by(rows_of(hT, w3cat[:, :], 0, D + 2, 3, turned_out(5)))
                pe.wait_ge(lin_out.sem, lin_out.at(b, 2))
                s_rows(H1, w3cat, D, 0)
                top_across(1, 1)
                for t in range(NT):
                    ins = pe.matmul(ps[:, 3, 0:F3], ones[:, 0:P], v3[:, t, 0, :], start=(t == 0),
                                    stop=(t == NT - 1))
                csum_ps.by(ins)
                if not last:
                    pe.wait_ge(args_ready.sem, args_ready.at(b, 2))
                    early_turn(b, 1)
                    early_projections(b, 1)
                    pe.wait_ge(v_ready.sem, v_ready.next(b, 1, 1))
                pe.wait_ge(ra_ready.sem, ra_ready.at(b, 2))
                for it in range(NT):
                    if it >= 2:
                        pe.wait_ge(t3_out.sem, t3_out.at(b, it - 1))
                    for s in range(2):
                        if it == 0 and s == 1:
                            pe.wait_ge(rb_ready.sem, rb_ready.at(b, 3))
                        for jt in range(NT):
                            if it == 0 and s == 0:
                                pe.wait_ge(step_ready.sem, step_ready.at(b, NT * H1 + jt + 1))
                            if it == 0 and s == 1:
                                pe.wait_ge(rest_ready.sem, rest_ready.at(b, jt + 1))
                            src = (step, rest)[s]
                            ins = pe.matmul(ps[:, 4 + 2 * (it % 2) + s, 0:3 * F3], src[:, jt, it * P:(it + 1) * P],
                                            r3[:, jt, 0, s, :, :].rearrange("p r f -> p (r f)"),
                                            start=(jt == 0), stop=(jt == NT - 1))
                    t3_ps.by(ins)

            early_turn(0, 0)
            early_projections(0, 0)
            if B > 1:
                with pe.Fori(0, B - 1) as b:
                    batch(b, False)
            batch(B - 1, True)

        copies = 2 if B > 1 else 1
        for s in signals:
            if s.per and s.given != s.per * copies:
                raise ValueError(f"{s.name}: {s.given} increments in {copies} batches, {s.per} a batch stated")


DVE_CHAIN, POOL_CHAIN = 150, 41
setup_marks = {}

_INS = ["x", "adj"] + ["L0_gnn_" + n for n in ("Wq", "bq", "Wk", "bk", "Wv", "bv", "Wo", "bo", "gamma", "beta")] + [
    "L1_gnn_" + n for n in ("W", "a_src", "a_dst", "beta_tilde", "W_out")] + [
    "L2_gnn_" + n for n in ("w_qkv", "ln1_g", "ln1_b", "ln2_g", "ln2_b", "w1", "b1", "w2", "b2")] + [
    "L3_gnn_" + n for n in ("W", "a")]


def kernel(**inputs):
    import numpy as np
    import concourse.bacc as bacc
    from concourse.bass_utils import run_bass_kernel_spmd

    nc = bacc.Bacc("TRN2", target_bir_lowering=False, num_devices=1)
    arrays, aps = {}, {}
    for name in _INS:
        a = np.ascontiguousarray(inputs[name])
        if a.ndim == 0:
            a = a.reshape(1)
        arrays[f"in_{name}"] = a
        aps[name] = nc.dram_tensor(f"in_{name}", a.shape, mybir.dt.from_np(a.dtype), kind="ExternalInput").ap()
    out = nc.dram_tensor("out_x", inputs["x"].shape, F32, kind="ExternalOutput").ap()
    program(nc, aps["x"], aps["adj"], aps, out, inputs["x"].shape[0])
    r = run_bass_kernel_spmd(nc, [arrays], core_ids=[0])
    return r.results[0]["out_x"]
```
